# Optimizing a Trainium2 kernel written in Bass

```python
import numpy as np
import jax
import jax.numpy as jnp

def _softmax(x, axis=-1):
    return jax.nn.softmax(x, axis=axis)

def _gelu(x):
    return jax.nn.gelu(x, approximate=True)

def _silu(x):
    return jax.nn.silu(x)

def _sigmoid(x):
    return jax.nn.sigmoid(x)

def _layernorm(x, axis=-1, eps=1e-05):
    m = jnp.mean(x, axis=axis, keepdims=True)
    v = jnp.var(x, axis=axis, keepdims=True)
    return (x - m) / jnp.sqrt(v + eps)

def _scatter_add(tgt, idx, src, axis=0):
    return tgt.at[idx].add(src)

def _segment_sum(src, seg, n):
    return jax.ops.segment_sum(src, seg, n)
kernel_name = 'mk_xattn_ffn_d2_seqx_r8_0669b1'

def setup_inputs(seed: int=0):
    np.random.seed(seed)
    _w = jnp.asarray

    def _rec_inputs():
        import jax
        import jax.numpy as jnp
        _rk = jax.random.key(seed)
        x = -0.0003929 + 0.9999 * jax.random.normal(jax.random.fold_in(_rk, 1), (2, 512, 128), jnp.float32)
        _lenS = 512 - jax.random.randint(jax.random.fold_in(_rk, 7), (2,), 0, max(1, 512 // 4) + 1, jnp.int32)
        _lenS2 = 32 - jax.random.randint(jax.random.fold_in(_rk, 8), (2,), 0, max(1, 32 // 4) + 1, jnp.int32)
        _ctx_1024P = jax.random.normal(jax.random.fold_in(_rk, 11), (2, 16, 128), jnp.float32)
        _ctx_1024c = jax.random.dirichlet(jax.random.fold_in(_rk, 511), 0.3 * jnp.ones((16,), jnp.float32), (2, 32))
        _ctx_1024t = jnp.einsum('bsk,bkd->bsd', _ctx_1024c, _ctx_1024P)
        _ctx_1024t = _ctx_1024t * jax.lax.rsqrt(jnp.mean(jnp.square(_ctx_1024t)) + 1e-12) * 0.953939
        ctx_1024 = 2.81802e-05 + 1.00001 * (_ctx_1024t + 0.3 * jax.random.normal(jax.random.fold_in(_rk, 611), (2, 32, 128), jnp.float32))
        _validS = jnp.arange(512)[None, :] < _lenS[:, None]
        _validS2 = jnp.arange(32)[None, :] < _lenS2[:, None]
        _causal = jnp.tril(jnp.ones((512, 512), dtype=bool))
        mask_BxS2_bf0 = jnp.logical_not(jnp.ones((2, 32), dtype=bool))
        return (x, ctx_1024, mask_BxS2_bf0)
    x, ctx_1024, mask_BxS2_bf0 = _rec_inputs()

    def _L0_xattn_setup():
        import jax, jax.numpy as jnp
        import numpy as np
        B, LQ, LKV, D = (8, 256, 256, 128)
        key = jax.random.key(seed)
        k1, k2, k3, k4, k5, k6, k7 = jax.random.split(key, 7)
        s = 1.0 / np.sqrt(D)
        return {'query': jax.random.normal(k1, (B, LQ, D), jnp.float32), 'key': jax.random.normal(k2, (B, LKV, D), jnp.float32), 'value': jax.random.normal(k3, (B, LKV, D), jnp.float32), 'Wq': jax.random.uniform(k4, (D, D), jnp.float32, -s, s), 'bq': jax.random.uniform(k5, (D,), jnp.float32, -s, s), 'Wk': jax.random.uniform(k6, (D, D), jnp.float32, -s, s), 'bk': jax.random.uniform(k7, (D,), jnp.float32, -s, s), 'scale_factor': 32, 'dropout_p': 0}
    _L0_xattn_all = _L0_xattn_setup()
    _L0_xattn_in = {k: v for k, v in _L0_xattn_all.items() if k in ('Wq', 'bq', 'Wk', 'bk')}
    del _L0_xattn_all

    def _L0_ffn_setup():
        import jax, jax.numpy as jnp
        import numpy as np
        from functools import partial
        HEADS = 16
        EPS = 1e-12

        def _l2_normalize(z):
            n = jnp.linalg.norm(z, axis=-1, keepdims=True)
            return z / jnp.maximum(n, EPS)
        key = jax.random.key(seed)
        kx, kq, kk, kv, ko, kf = jax.random.split(key, 6)
        B, S, D, L = (2, 256, 128, 128)
        scale = 0.02
        return {'x': jax.random.normal(kx, (B, S, D), dtype=jnp.float32), 'Wq': jax.random.normal(kq, (D, L), dtype=jnp.float32) * scale, 'Wk': jax.random.normal(kk, (D, L), dtype=jnp.float32) * scale, 'Wv': jax.random.normal(kv, (D, L), dtype=jnp.float32) * scale, 'Wo': jax.random.normal(ko, (L, D), dtype=jnp.float32) * scale, 'Wff': jax.random.normal(kf, (D, D), dtype=jnp.float32) * scale}
    _L0_ffn_all = _L0_ffn_setup()
    _L0_ffn_in = {k: v for k, v in _L0_ffn_all.items() if k in ('Wq', 'Wk', 'Wv', 'Wo', 'Wff')}
    del _L0_ffn_all

    def _L1_xattn_setup():
        import jax, jax.numpy as jnp
        import numpy as np
        B, L1, L2, FULL, H = (8, 256, 256, 128, 128)
        NEG_INF = -1e+30
        key = jax.random.key(seed)
        k1, k2, k3, k4, k5 = jax.random.split(key, 5)
        xh1 = jax.random.normal(k1, (B, L1, FULL), dtype=jnp.float32)
        xh2 = jax.random.normal(k2, (B, L2, FULL), dtype=jnp.float32)
        x2 = jax.random.normal(k3, (B, L2, H), dtype=jnp.float32)
        x2_mask = jnp.zeros((B, L2), dtype=bool)
        W = jax.random.normal(k4, (FULL, FULL), dtype=jnp.float32) / np.sqrt(FULL)
        b = jnp.zeros((FULL,), dtype=jnp.float32)
        D = jnp.ones((1, FULL), dtype=jnp.float32)
        return {'xh1': xh1, 'xh2': xh2, 'x2': x2, 'x2_mask': x2_mask, 'W': W, 'b': b, 'D': D}
    _L1_xattn_all = _L1_xattn_setup()
    _L1_xattn_in = {k: v for k, v in _L1_xattn_all.items() if k in ('W', 'b', 'D')}
    del _L1_xattn_all

    def _L1_ffn_setup():
        import jax, jax.numpy as jnp
        import numpy as np
        from jax import lax
        B, N, D, H, E, K = (16, 128, 128, 512, 8, 2)
        key = jax.random.key(seed)
        ks = jax.random.split(key, 12)
        s = 0.02
        return {'x': jax.random.normal(ks[0], (B, N, D), jnp.float32), 'alpha': jnp.asarray(0.9, jnp.float32), 'w_gate': jax.random.normal(ks[1], (D, E), jnp.float32) * s, 'b_gate': jnp.zeros((E,), jnp.float32), 'W1m': jax.random.normal(ks[2], (D, H), jnp.float32) * s, 'b1m': jnp.zeros((H,), jnp.float32), 'W2m': jax.random.normal(ks[3], (H, D), jnp.float32) * s, 'b2m': jnp.zeros((D,), jnp.float32), 'W1e': jax.random.normal(ks[4], (E, D, H), jnp.float32) * s, 'b1e': jnp.zeros((E, H), jnp.float32), 'W2e': jax.random.normal(ks[5], (E, H, D), jnp.float32) * s, 'b2e': jnp.zeros((E, D), jnp.float32)}
    _L1_ffn_all = _L1_ffn_setup()
    _L1_ffn_in = {k: v for k, v in _L1_ffn_all.items() if k in ('alpha', 'w_gate', 'b_gate', 'W1m', 'b1m', 'W2m', 'b2m', 'W1e', 'b1e', 'W2e', 'b2e')}
    del _L1_ffn_all
    return {'x': x, 'ctx_1024': ctx_1024, 'mask_BxS2_bf0': mask_BxS2_bf0, 'L0_xattn_Wq': _L0_xattn_in['Wq'], 'L0_xattn_bq': _L0_xattn_in['bq'], 'L0_xattn_Wk': _L0_xattn_in['Wk'], 'L0_xattn_bk': _L0_xattn_in['bk'], 'L0_ffn_Wq': _L0_ffn_in['Wq'], 'L0_ffn_Wk': _L0_ffn_in['Wk'], 'L0_ffn_Wv': _L0_ffn_in['Wv'], 'L0_ffn_Wo': _L0_ffn_in['Wo'], 'L0_ffn_Wff': _L0_ffn_in['Wff'], 'L1_xattn_W': _L1_xattn_in['W'], 'L1_xattn_b': _L1_xattn_in['b'], 'L1_xattn_D': _L1_xattn_in['D'], 'L1_ffn_alpha': _L1_ffn_in['alpha'], 'L1_ffn_w_gate': _L1_ffn_in['w_gate'], 'L1_ffn_b_gate': _L1_ffn_in['b_gate'], 'L1_ffn_W1m': _L1_ffn_in['W1m'], 'L1_ffn_b1m': _L1_ffn_in['b1m'], 'L1_ffn_W2m': _L1_ffn_in['W2m'], 'L1_ffn_b2m': _L1_ffn_in['b2m'], 'L1_ffn_W1e': _L1_ffn_in['W1e'], 'L1_ffn_b1e': _L1_ffn_in['b1e'], 'L1_ffn_W2e': _L1_ffn_in['W2e'], 'L1_ffn_b2e': _L1_ffn_in['b2e']}

def reference(x, ctx_1024, mask_BxS2_bf0, L0_xattn_Wq, L0_xattn_bq, L0_xattn_Wk, L0_xattn_bk, L0_ffn_Wq, L0_ffn_Wk, L0_ffn_Wv, L0_ffn_Wo, L0_ffn_Wff, L1_xattn_W, L1_xattn_b, L1_xattn_D, L1_ffn_alpha, L1_ffn_w_gate, L1_ffn_b_gate, L1_ffn_W1m, L1_ffn_b1m, L1_ffn_W2m, L1_ffn_b2m, L1_ffn_W1e, L1_ffn_b1e, L1_ffn_W2e, L1_ffn_b2e):
    import jax
    import jax.numpy as jnp

    def _L0_xattn_ref(query, key, value, Wq, bq, Wk, bk, scale_factor, dropout_p):
        import jax, jax.numpy as jnp
        import numpy as np
        B, LQ, LKV, D = (8, 256, 256, 128)
        q = jnp.einsum('bld,ed->ble', query, Wq) + bq
        k = jnp.einsum('bld,ed->ble', key, Wk) + bk
        scores = jnp.einsum('bqd,bkd->bqk', q, k) / jnp.float32(scale_factor)
        attn = jax.nn.softmax(scores, axis=-1)
        return jnp.einsum('bqk,bkd->bqd', attn, value)

    def _L0_ffn_ref(x, Wq, Wk, Wv, Wo, Wff):
        import jax, jax.numpy as jnp
        import numpy as np
        from functools import partial
        HEADS = 16
        EPS = 1e-12

        def _l2_normalize(z):
            n = jnp.linalg.norm(z, axis=-1, keepdims=True)
            return z / jnp.maximum(n, EPS)
        B, S, D = x.shape
        H = HEADS
        L = Wq.shape[1]
        dh = L // H

        def split_heads(t):
            return t.reshape(B, S, H, dh).transpose(0, 2, 1, 3).reshape(B * H, S, dh)
        q = split_heads(x @ Wq)
        k = split_heads(x @ Wk)
        v = split_heads(x @ Wv)
        scores = jnp.einsum('bqd,bkd->bkq', q, k) / jnp.sqrt(jnp.asarray(D, x.dtype))
        attn = jax.nn.softmax(scores, axis=-1)
        out = jnp.einsum('bkq,bkv->bqv', attn, v)
        z = out.reshape(B, H, S, dh).transpose(0, 2, 1, 3).reshape(B, S, L)
        z = z @ Wo
        z = _l2_normalize(z)
        z = z @ Wff
        z = _l2_normalize(z)
        z = jax.nn.gelu(z, approximate=False)
        return z

    def _L1_xattn_ref(xh1, xh2, x2, x2_mask, W, b, D):
        import jax, jax.numpy as jnp
        import numpy as np
        B, L1, L2, FULL, H = (8, 256, 256, 128, 128)
        NEG_INF = -1e+30
        x1_key = jax.nn.relu(jnp.einsum('bsf,fg->bsg', xh1, W.T) + b)
        x2_key = jax.nn.relu(jnp.einsum('btf,fg->btg', xh2, W.T) + b)
        x2_key = x2_key * D[None, :, :]
        scores = jnp.einsum('bsf,btf->bst', x1_key, x2_key)
        scores = jnp.where(x2_mask[:, None, :], NEG_INF, scores)
        alpha = jax.nn.softmax(scores, axis=-1)
        seq_ave = jnp.einsum('bst,bth->bsh', alpha, x2)
        return seq_ave

    def _L1_ffn_ref(x, alpha, w_gate, b_gate, W1m, b1m, W2m, b2m, W1e, b1e, W2e, b2e):
        import jax, jax.numpy as jnp
        import numpy as np
        from jax import lax
        B, N, D, H, E, K = (16, 128, 128, 512, 8, 2)
        main = jax.nn.gelu(x @ W1m + b1m) @ W2m + b2m
        logits = jnp.mean(x, axis=1) @ w_gate + b_gate
        probs = jax.nn.softmax(logits, axis=-1)
        top_vals, top_idx = lax.top_k(probs, K)
        gate_w = top_vals / jnp.sum(top_vals, axis=-1, keepdims=True)
        W1g = W1e[top_idx]
        b1g = b1e[top_idx]
        W2g = W2e[top_idx]
        b2g = b2e[top_idx]
        h = jax.nn.gelu(jnp.einsum('bnd,bkdh->bknh', x, W1g) + b1g[:, :, None, :])
        eo = jnp.einsum('bknh,bkhd->bknd', h, W2g) + b2g[:, :, None, :]
        expert_out = jnp.einsum('bk,bknd->bnd', gate_w, eo)
        a = jnp.clip(alpha, 0.1, 1.0)
        return a * main + (1.0 - a) * expert_out
    x = x + _L0_xattn_ref(_layernorm(x, axis=-1), ctx_1024, ctx_1024, L0_xattn_Wq, L0_xattn_bq, L0_xattn_Wk, L0_xattn_bk, 32, 0)
    x = x + _L0_ffn_ref(_layernorm(x, axis=-1), L0_ffn_Wq, L0_ffn_Wk, L0_ffn_Wv, L0_ffn_Wo, L0_ffn_Wff)
    x = x + _L1_xattn_ref(_layernorm(x, axis=-1), ctx_1024, ctx_1024, mask_BxS2_bf0, L1_xattn_W, L1_xattn_b, L1_xattn_D)
    x = x + _L1_ffn_ref(_layernorm(x, axis=-1), L1_ffn_alpha, L1_ffn_w_gate, L1_ffn_b_gate, L1_ffn_W1m, L1_ffn_b1m, L1_ffn_W2m, L1_ffn_b2m, L1_ffn_W1e, L1_ffn_b1e, L1_ffn_W2e, L1_ffn_b2e)
    return x

_drawn_inputs = setup_inputs


def setup_inputs(seed=0):
    import zlib

    import numpy as np

    out = dict(_drawn_inputs(seed))
    spreads = {'L1_xattn_b': (0.0, 0.1),
     'L1_xattn_D': (1.0, 0.2),
     'L1_ffn_b_gate': (0.0, 0.8),
     'L1_ffn_b1m': (0.0, 0.659),
     'L1_ffn_b2m': (0.0, 0.1),
     'L1_ffn_b1e': (0.0, 0.8),
     'L1_ffn_b2e': (0.0, 0.8)}
    factors = {'L0_xattn_bq': 8.0,
     'L0_xattn_bk': 64.0,
     'L0_ffn_Wq': 31.665,
     'L0_ffn_Wk': 28.599,
     'L1_ffn_w_gate': 8.0,
     'L1_ffn_W1e': 8.0,
     'L1_ffn_W2e': 8.0}
    for name, (base, spread) in spreads.items():
        noise = np.random.default_rng([zlib.crc32(name.encode()), seed]).standard_normal(out[name].shape)
        drawn = base * np.exp(spread * noise) if base else spread * noise
        out[name] = jnp.asarray(drawn.astype(out[name].dtype))
    for name, factor in factors.items():
        out[name] = (out[name] * factor).astype(out[name].dtype)
    return out
```

```python
from contextlib import ExitStack

import concourse.bass as bass
from concourse import mybir

ALU = mybir.AluOpType
ACT = mybir.ActivationFunctionType
F32 = mybir.dt.float32
BF16 = mybir.dt.bfloat16
U32 = mybir.dt.uint32
AX = mybir.AxisListType

P = 128
B, S, D = 2, 512, 128
T = S // P
KV = 32
HEADS, DH = 16, 8
G, J = 4, 4
E, H, C = 8, 512, 4
NETS = 3
LN_EPS = 1e-5
PARTS = 3
SLOTS = PARTS * PARTS - 1
ROWS = SLOTS * DH
NSC = 4
NE = 24
QUADS = B * G * T
PV_LAG = T + 1

FIRST = dict(wkT=(0, 128), wq0=(128, 128), ctxT=(256, 64), bk=(320, 1), bq=(321, 1))
FIRST_N = 322
REST = dict(wq=(0, 128), wk=(128, 128), wv=(256, 128), wo=(384, 128), woT=(512, 128), wff=(640, 128),
            wxT=(768, 128), wg=(896, E), bx=(904, 1), dx=(905, 1), b1=(906, (E + 1) * C))
REST_N = 906 + (E + 1) * C


def block_kernel(nc, x, ctx, first, rest, w1m, w1e, w2m, w2e, b2, row, mask, out):
    with ExitStack() as stack:
        def sb(name, shape, dt=F32):
            return stack.enter_context(nc.sbuf_tensor(name, shape, dt))

        def sem(name):
            return stack.enter_context(nc.semaphore(name))

        bank = [stack.enter_context(nc.psum_tensor(f"bank{i}", [P, 512], F32)) for i in range(8)]

        ident = sb("ident", [P, P])
        minus_half = sb("minus_half", [P, T])
        iota_u = sb("iota_u", [P, E], mybir.dt.int32)
        iota_f = sb("iota_f", [P, E])
        first_sb = sb("first_sb", [P, FIRST_N])
        rest_sb = sb("rest_sb", [P, REST_N])
        ctx_bd = sb("ctx_bd", [P, B, T, D])
        w1 = sb("w1", [P, (E + 1) * H])
        w2 = sb("w2", [P, (E + 1) * H])
        b2_sb = sb("b2_sb", [E + 1, D])
        row_sb = sb("row_sb", [P, E + 1])
        mask_sb = sb("mask_sb", [P, B * KV], mybir.dt.int32)
        mask_bias = sb("mask_bias", [P, B * KV])
        a_sb = sb("a_sb", [P, 2])
        w2_main = sb("w2_main", [P, H])
        wof = sb("wof", [P, 2 * D])
        key0 = sb("key0", [P, B * KV])
        fold = sb("fold", [P, 2 * B * KV])
        key2 = sb("key2", [P, B * KV])

        def fw(name):
            at, n = FIRST[name]
            return first_sb[:, at:at + n]

        def rw(name):
            at, n = REST[name]
            return rest_sb[:, at:at + n]

        xr = sb("xr", [P, B, T, D])
        xn = sb("xn", [P, B, T, D])
        xT = sb("xT", [P, B, S])
        x3T = xn[:].rearrange("p b t d -> p b (t d)")
        stats = sb("stats", [P, B, T, 6])
        mv = sb("mv", [P, B, T, 2])
        veps = sb("veps", [P, B, T])
        rstd = sb("rstd", [P, B, T])
        sm = sb("sm", [P, B, T, KV])
        smx = sb("smx", [P, B, T])
        pr = sb("pr", [P, B, T, KV])
        prT = sb("prT", [P, B, P])
        keyT = sb("keyT", [P, B, S])
        early = sb("early", [P, 2, B, 2, S])
        qk, qkr = early[:, 0], early[:, 1]
        w1s, w2s = early[:, 0], early[:, 1]
        parts = sb("parts", [P, B * 2 * PARTS * S], BF16)
        qkp = parts[:].rearrange("p (b w c s) -> p b w c s", b=B, w=2, c=PARTS)
        hid = parts[:, 0:4 * 2 * S].bitcast(F32).rearrange("p (u s) -> p u s", u=4)
        qs = sb("qs", [B * ROWS, HEADS, S], BF16)
        ks = sb("ks", [B * ROWS, HEADS, S], BF16)
        v = sb("v", [P, B, T, J, KV])
        vn = sb("vn", [P, G, T * J, KV])
        ex = sb("ex", [P, NE, S])
        neg_max = sb("neg_max", [P, QUADS * J])
        sums = sb("sums", [P, QUADS * J])
        rsum = sb("rsum", [P, QUADS * J])
        oT = parts[:, 4 * 2 * S:].bitcast(F32).rearrange("p (b s) -> p b s", b=B)
        sq = early[:, 1].rearrange("p b w (a d) -> p (b w a) d", d=D)[:, 0:2 * T]
        ss = sb("ss", [P, B, T, 2])
        farg = sb("farg", [P, B, 2, T])
        fz = sb("fz", [P, B, T])
        gz = early[:, 0].rearrange("p b w (a d) -> p b (w a) d", d=D)[:, :, 0:T]
        xsum = sb("xsum", [P, B])
        logit = sb("logit", [P, B, E])
        lmax = sb("lmax", [P, B, 2])
        prob = sb("prob", [P, B, E])
        top = sb("top", [P, B, 8])
        top_i = sb("top_i", [P, B, 8], U32)
        top_f = sb("top_f", [P, B, 2])
        gate = sb("gate", [P, B, 4])
        coef = sb("coef", [P, B, E + 1])
        coef2 = sb("coef2", [P, B, E])
        coefT = sb("coefT", [E + 1, B, P])
        b1s = sb("b1s", [P, B, 2, C])
        res = xT[:].rearrange("p b (t d) -> p b t d", t=T)

        ld_first, ld_rest, ld_small = sem("ld_first"), sem("ld_rest"), sem("ld_small")
        ld_ctx, ld_w1, ld_w2, ld_b2 = sem("ld_ctx"), sem("ld_w1"), sem("ld_w2"), sem("ld_b2")
        ld_x = [sem(f"ld_x{b}") for b in range(B)]
        st_out = sem("st_out")
        const_done = sem("const_done")
        bd_zero = sem("bd_zero")
        pool_step = sem("pool_step")
        v_step = sem("v_step")
        a_step = sem("a_step")
        keys_mm, key0_done, fold_mm, fold_done, key2_mm, key2_done, wof_mm, prep_done = (
            sem(n) for n in ("keys_mm", "key0_done", "fold_mm", "fold_done", "key2_mm", "key2_done",
                             "wof_mm", "prep_done"))
        KINDS = ("cross0", "self", "cross1", "ffn")
        var_done = {k: sem(f"var_{k}") for k in KINDS}
        rstd_done = {k: sem(f"rstd_{k}") for k in KINDS}
        xn_done = {k: sem(f"xn_{k}") for k in KINDS}
        xT_mm = {k: sem(f"xT_mm_{k}") for k in KINDS}
        xT_done = {k: sem(f"xT_{k}") for k in KINDS}
        CROSS = ("cross0", "cross1")
        sc_mm = {k: sem(f"sc_mm_{k}") for k in CROSS}
        shifted = {k: sem(f"shifted_{k}") for k in CROSS}
        expd = {k: sem(f"expd_{k}") for k in CROSS}
        pr_done = {k: sem(f"pr_{k}") for k in CROSS}
        prT_mm = {k: sem(f"prT_mm_{k}") for k in CROSS}
        prT_done = {k: sem(f"prT_{k}") for k in CROSS}
        av_mm = {k: sem(f"av_mm_{k}") for k in CROSS}
        x_done = {k: sem(f"x_{k}") for k in CROSS}
        key_mm, key_done = sem("key_mm"), sem("key_done")
        q_mm, k_mm, v_mm = sem("q_mm"), sem("k_mm"), sem("v_mm")
        qk_done, p1_done, r1_done, p2_done, p3_done = (
            sem(n) for n in ("qk_done", "p1_done", "r1_done", "p2_done", "p3_done"))
        v_done = sem("v_done")
        q_stacked = [sem(f"q_stacked{b}") for b in range(B)]
        k_stacked = [sem(f"k_stacked{b}") for b in range(B)]
        score_mm, max_done, exp_done, vn_done, pv_done = (
            sem(n) for n in ("score_mm", "max_done", "exp_done", "vn_done", "pv_done"))
        oT_done, z_mm, sq_done, farg_done, fz_done, gelu_done = (
            sem(n) for n in ("oT_done", "z_mm", "sq_done", "farg_done", "fz_done", "gelu_done"))
        logit_mm, logit_done, pexp_done, coef_done, coefT_mm, coefT_done, chosen = (
            sem(n) for n in ("logit_mm", "logit_done", "pexp_done", "coef_done", "coefT_mm",
                             "coefT_done", "chosen"))
        hid_mm, hid_done, hid_used, acc_mm, res_done = (
            sem(n) for n in ("hid_mm", "hid_done", "hid_used", "acc_mm", "res_done"))

        T_BANK = {"cross0": (0, 3), "self": (0, 3), "cross1": (4, 5), "ffn": (4, 5)}
        S_BANK = {"cross0": (1, 4), "cross1": (7, 1)}
        O_BANK = {"cross0": (2, 5), "cross1": (6, 0)}
        Q_BANK, K_BANK, V_BANK = (1, 4), (2, 5), (6, 7)
        OT_BANK = (4, 5)
        Z_BANK = ((6, 7), (0, 1))
        KEY_BANK = (6, 0)
        GATE_BANK = (7, 1)
        H_BANK = ((6, 7), (0, 1))
        ACC_BANK = (4, 5)

        def tile_of(i):
            return i // (G * T * J), i // (T * J) % G, i // J % T, i % J

        block = stack.enter_context(nc.Block())

        @block.sync
        def _(sp):
            sp.dma_start(xr[:, 0], x[0].rearrange("(t p) d -> p t d", p=P)).then_inc(ld_x[0], 16)
            sp.dma_start(first_sb[:], first).then_inc(ld_first, 16)
            sp.dma_start(xr[:, 1], x[1].rearrange("(t p) d -> p t d", p=P)).then_inc(ld_x[1], 16)
            sp.wait_ge(bd_zero, 1)
            for t in range(T):
                sp.dma_start(ctx_bd[KV * t:KV * t + KV, :, t, :],
                             ctx.rearrange("b k d -> k b d")).then_inc(ld_ctx, 16)
            sp.dma_start(rest_sb[:], rest).then_inc(ld_rest, 16)
            sp.dma_start(row_sb[:], row.broadcast_to([P, E + 1])).then_inc(ld_small, 16)
            sp.dma_start(mask_sb[:], mask.broadcast_to([P, B * KV])).then_inc(ld_small, 16)
            sp.dma_start(b2_sb[:], b2).then_inc(ld_b2, 16)
            for b in range(B):
                for part, done in ((0, p1_done), (1, p2_done), (2, p3_done)):
                    sp.wait_ge(done, 2 * b + 1)
                    for other in range(PARTS if part < 2 else PARTS - 1):
                        r = ROWS * b + (PARTS * part + other) * DH
                        sp.dma_start(qs[r:r + DH], qkp[:, b, 0, part]).then_inc(q_stacked[b], 16)
            sp.dma_start(w1[:, 0:H], w1m).then_inc(ld_w1, 16)
            sp.dma_start(w1[:, H:].rearrange("d (e h) -> d e h", e=E),
                         w1e.rearrange("e d h -> d e h")).then_inc(ld_w1, 16)
            sp.dma_start(w2[:, 0:H].rearrange("p (c d) -> p c d", c=C),
                         w2m.rearrange("(c p) d -> p c d", p=P)).then_inc(ld_w2, 16)
            sp.dma_start(w2[:, H:].rearrange("p (e d) -> p e d", e=E * C),
                         w2e.rearrange("e (c p) d -> p (e c) d", p=P)).then_inc(ld_w2, 16)
            for b in range(B):
                sp.wait_ge(res_done, b + 1)
                sp.dma_start(out[b].rearrange("(t p) d -> p t d", p=P), res[:, b]).then_inc(st_out, 16)
            sp.wait_ge(st_out, 16 * B)

        @block.gpsimd
        def _(pool):
            nc.gpsimd.memset(minus_half[:], -0.5)
            nc.gpsimd.memset(ident[:], 0.0).then_inc(pool_step, 1)
            nc.gpsimd.memset(ctx_bd[:], 0.0).then_inc(bd_zero, 1)
            pool.wait_ge(pool_step, 1)
            nc.gpsimd.affine_select(out=ident[:], in_=ident[:], compare_op=ALU.not_equal, fill=1.0, base=0,
                                    pattern=[[-1, P]], channel_multiplier=1).then_inc(const_done, 1)
            nc.gpsimd.iota(iota_u[:], pattern=[[1, E]], base=0, channel_multiplier=0).then_inc(const_done, 1)

            def rstd_of(kind, b):
                pool.wait_ge(var_done[kind], b + 1)
                nc.gpsimd.tensor_tensor(rstd[:, b], veps[:, b], minus_half[:], ALU.pow).then_inc(rstd_done[kind], 1)

            rstd_of("cross0", 0)
            nc.gpsimd.memset(vn[:], 0.0).then_inc(const_done, 1)
            rstd_of("cross0", 1)
            rstd_of("self", 0)
            rstd_of("self", 1)
            for b in range(B):
                for part, done in ((0, p1_done), (1, p2_done), (2, p3_done)):
                    pool.wait_ge(done, 2 * b + 2)
                    for other in range(PARTS if part < 2 else PARTS - 1):
                        r = ROWS * b + (PARTS * other + part) * DH
                        pool.dma_start(ks[r:r + DH], qkp[:, b, 1, part]).then_inc(k_stacked[b], 16)
            for b in range(B):
                pool.wait_ge(farg_done, b + 1)
                nc.gpsimd.tensor_tensor(fz[:, b], farg[:, b, 1], minus_half[:], ALU.pow).then_inc(fz_done, 1)
                rstd_of("cross1", b)
            for b in range(B):
                rstd_of("ffn", b)

        @block.scalar
        def _(act):
            def copy_xT(kind, b):
                act.wait_ge(xT_mm[kind], b + 1)
                src = bank[T_BANK[kind][b]][:]
                if kind == "ffn":
                    nc.scalar.activation(x3T[:, b], src, ACT.Copy,
                                         accum_out=xsum[:, b:b + 1]).then_inc(xT_done[kind], 1)
                else:
                    nc.scalar.activation(xT[:, b], src, ACT.Copy).then_inc(xT_done[kind], 1)

            def cross_exp(kind, b):
                act.wait_ge(shifted[kind], b + 1)
                nc.scalar.activation(pr[:, b], sm[:, b], ACT.Exp).then_inc(expd[kind], 1)

            def cross_prT(kind, b):
                act.wait_ge(prT_mm[kind], b + 1)
                nc.scalar.activation(prT[:, b], bank[S_BANK[kind][b]][:, P:2 * P], ACT.Copy).then_inc(prT_done[kind], 1)

            def split(b):
                for which, ready, src in ((0, q_mm, Q_BANK), (1, k_mm, K_BANK)):
                    act.wait_ge(ready, b + 1)
                    scale = -float(D) ** -0.5 if which == 0 else 1.0
                    nc.scalar.activation(qk[:, b, which], bank[src[b]][:], ACT.Copy, scale=scale).then_inc(qk_done, 1)
                    act.wait_ge(qk_done, 2 * b + which + 1)
                    nc.scalar.activation(qkp[:, b, which, 0], qk[:, b, which], ACT.Copy).then_inc(p1_done, 1)
                for which in range(2):
                    act.wait_ge(r1_done, 2 * b + which + 1)
                    nc.scalar.activation(qkp[:, b, which, 1], qkr[:, b, which], ACT.Copy).then_inc(p2_done, 1)

            for b in range(B):
                copy_xT("cross0", b)
            for b in range(B):
                cross_exp("cross0", b)
            for b in range(B):
                cross_prT("cross0", b)
            for b in range(B):
                copy_xT("self", b)
            for b in range(B):
                split(b)
                act.wait_ge(v_mm, b + 1)
                nc.scalar.activation(v[:, b].rearrange("p t j c -> p (t j c)"), bank[V_BANK[b]][:], ACT.Copy).then_inc(v_done, 1)

            for i in range(QUADS * J):
                act.wait_ge(max_done, i + 1)
                if i >= NE:
                    act.wait_ge(pv_done, (i - NE) // J + 1)
                nc.scalar.activation(ex[:, i % NE], bank[i % NSC][:], ACT.Exp, bias=neg_max[:, i:i + 1], scale=-1.0,
                                     accum_out=sums[:, i:i + 1]).then_inc(exp_done, 1)

            def squares(b):
                act.wait_ge(z_mm, b + 1)
                if b:
                    act.wait_ge(farg_done, b)
                for half in range(2):
                    nc.scalar.activation(sq[:, 4 * half:4 * half + 4].rearrange("p a d -> p (a d)"),
                                         bank[Z_BANK[b][half]][:], ACT.Square).then_inc(sq_done, 1)

            def gelu_z(b):
                act.wait_ge(fz_done, b + 1)
                for t in range(T):
                    at = (t % 2) * 2 * D + D
                    nc.scalar.activation(gz[:, b, t], bank[Z_BANK[b][t // 2]][:, at:at + D], ACT.Gelu,
                                         scale=fz[:, b, t:t + 1]).then_inc(gelu_done, 1)

            def relu_key(b):
                act.wait_ge(key_mm, b + 1)
                nc.scalar.activation(keyT[:, b], bank[KEY_BANK[b]][:], ACT.Relu, bias=rw("bx")).then_inc(key_done, 1)

            def gate_exp(b):
                act.wait_ge(logit_done, b + 1)
                nc.scalar.activation(prob[:, b], logit[:, b], ACT.Exp, bias=lmax[:, b, 0:1],
                                     accum_out=lmax[:, b, 1:2]).then_inc(pexp_done, 1)

            for b in range(B):
                squares(b)
            for b in range(B):
                gelu_z(b)
            for b in range(B):
                copy_xT("cross1", b)
                relu_key(b)
            for b in range(B):
                cross_exp("cross1", b)
            for b in range(B):
                cross_prT("cross1", b)
            for b in range(B):
                copy_xT("ffn", b)
                gate_exp(b)
                act.wait_ge(coefT_mm, b + 1)
                nc.scalar.activation(coefT[:, b], bank[GATE_BANK[b]][0:E + 1, P:2 * P], ACT.Copy).then_inc(coefT_done, 1)
            for u in range(B * NETS * C):
                b, net, c = u // (NETS * C), u // C % NETS, u % C
                act.wait_ge(hid_mm, u + 1)
                if u >= 4:
                    act.wait_ge(hid_used, u - 3)
                if net == 0:
                    bias = rw("b1")[:, c:c + 1]
                else:
                    act.wait_ge(chosen, b + 1)
                    bias = b1s[:, b, net - 1, c:c + 1]
                nc.scalar.activation(hid[:, u % 4], bank[H_BANK[b][u % 2]][:], ACT.Gelu_apprx_tanh,
                                     bias=bias).then_inc(hid_done, 1)

        @block.vector
        def _(dve):
            links = [0]

            def link(ins):
                links[0] += 1
                ins.then_inc(v_step, 1)
                dve.wait_ge(v_step, links[0])

            def layer_norm(kind, b):
                if kind == "cross0":
                    dve.wait_ge(ld_x[b], 16)
                for t in range(T):
                    last = nc.vector.bn_stats(stats[:, b, t], xr[:, b, t])
                link(last)
                for t in range(T):
                    last = nc.vector.bn_aggr(mv[:, b, t], stats[:, b, t])
                link(last)
                nc.vector.tensor_scalar(veps[:, b], mv[:, b, :, 1], LN_EPS, None, ALU.add).then_inc(var_done[kind], 1)

            def normalise(kind, b):
                dve.wait_ge(rstd_done[kind], b + 1)
                for t in range(T):
                    nc.vector.tensor_scalar(xn[:, b, t], xr[:, b, t], mv[:, b, t, 0:1], rstd[:, b, t:t + 1],
                                            ALU.subtract, ALU.mult).then_inc(xn_done[kind], 1)

            def softmax_in(kind, b):
                bias = fold[:, B * KV + KV * b:B * KV + KV * b + KV] if kind == "cross0" else mask_bias[:, KV * b:KV * b + KV]
                dve.wait_ge(sc_mm[kind], b + 1)
                ps = bank[S_BANK[kind][b]][:, 0:T * KV].rearrange("p (t k) -> p t k", t=T)
                link(nc.vector.tensor_tensor(sm[:, b], ps, bias.unsqueeze(1).broadcast_to([P, T, KV]), ALU.add))
                link(nc.vector.tensor_reduce(smx[:, b], sm[:, b], AX.X, ALU.max))
                nc.vector.tensor_tensor(sm[:, b], sm[:, b], smx[:, b].unsqueeze(2).broadcast_to([P, T, KV]),
                                        ALU.subtract).then_inc(shifted[kind], 1)

            def softmax_out(kind, b):
                dve.wait_ge(expd[kind], b + 1)
                link(nc.vector.tensor_reduce(smx[:, b], pr[:, b], AX.X, ALU.add))
                link(nc.vector.reciprocal(smx[:, b], smx[:, b]))
                nc.vector.tensor_tensor(pr[:, b], pr[:, b], smx[:, b].unsqueeze(2).broadcast_to([P, T, KV]),
                                        ALU.mult).then_inc(pr_done[kind], 1)

            def cross_add(kind, b):
                dve.wait_ge(av_mm[kind], b + 1)
                xf = xr[:, b].rearrange("p t d -> p (t d)")
                nc.vector.tensor_tensor(xf, bank[O_BANK[kind][b]][:], xf, ALU.add).then_inc(x_done[kind], 1)
                dve.wait_ge(x_done[kind], b + 1)

            def prep():
                dve.wait_ge(ld_first, 16)
                dve.wait_ge(keys_mm, 1)
                nc.vector.tensor_scalar(key0[:], bank[4][:, 0:B * KV], fw("bk"), 1.0 / 32.0,
                                        ALU.add, ALU.mult).then_inc(key0_done, 1)
                dve.wait_ge(fold_mm, 1)
                nc.vector.tensor_copy(fold[:], bank[7][:, 0:2 * B * KV]).then_inc(fold_done, 1)

            def prep_rest():
                dve.wait_ge(ld_rest, 16)
                dve.wait_ge(key2_mm, 1)
                link(nc.vector.tensor_scalar(key2[:], bank[5][:, 0:B * KV], rw("bx"), 0.0, ALU.add, ALU.max))
                nc.vector.tensor_scalar(key2[:], key2[:], rw("dx"), None, ALU.mult).then_inc(key2_done, 1)
                nc.vector.tensor_copy(wof[:, 0:D], rw("wo"))
                dve.wait_ge(wof_mm, 1)
                nc.vector.tensor_copy(wof[:, D:], bank[6][:, 0:D]).then_inc(prep_done, 1)
                dve.wait_ge(ld_small, 32)
                nc.vector.tensor_scalar(mask_bias[:], mask_sb[:], -1e30, None, ALU.mult)
                link(nc.vector.tensor_scalar(a_sb[:, 0:1], row_sb[:, E:E + 1], 0.1, 1.0, ALU.max, ALU.min))
                nc.vector.tensor_scalar(a_sb[:, 1:2], a_sb[:, 0:1], -1.0, 1.0, ALU.mult, ALU.add)
                dve.wait_ge(const_done, 3)
                link(nc.vector.tensor_copy(iota_f[:], iota_u[:]))

            def split(b):
                for which in range(2):
                    dve.wait_ge(p1_done, 2 * b + which + 1)
                    nc.vector.tensor_tensor(qkr[:, b, which], qk[:, b, which], qkp[:, b, which, 0],
                                            ALU.subtract).then_inc(r1_done, 1)
                for which in range(2):
                    dve.wait_ge(p2_done, 2 * b + which + 1)
                    nc.vector.tensor_tensor(qkp[:, b, which, 2], qkr[:, b, which], qkp[:, b, which, 1],
                                            ALU.subtract).then_inc(p3_done, 1)

            def score_max(quad):
                for i in range(J * quad, J * quad + J):
                    dve.wait_ge(score_mm, i + 1)
                    nc.vector.tensor_reduce(neg_max[:, i:i + 1], bank[i % NSC][:], AX.X, ALU.min).then_inc(max_done, 1)

            def norm_values(n):
                b, g = n // G, n % G
                if n == 0:
                    dve.wait_ge(v_done, 1)
                if g == 0 and b:
                    dve.wait_ge(v_done, b + 1)
                if n >= G:
                    dve.wait_ge(pv_done, T * (n - G + 1))
                a, z = T * J * n, T * J * (n + 1)
                dve.wait_ge(exp_done, z)
                link(nc.vector.reciprocal(rsum[:, a:z], sums[:, a:z]))
                nc.vector.tensor_tensor(vn[:, g, :, DH * g:DH * g + DH],
                                        v[:, b, :, :, DH * g:DH * g + DH].rearrange("p t j d -> p (t j) d"),
                                        rsum[:, a:z].unsqueeze(2).broadcast_to([P, T * J, DH]),
                                        ALU.mult).then_inc(vn_done, 1)

            def copy_oT(b):
                dve.wait_ge(pv_done, (b + 1) * G * T)
                nc.vector.tensor_copy(oT[:, b], bank[OT_BANK[b]][:]).then_inc(oT_done, 1)

            def norms(b):
                dve.wait_ge(sq_done, 2 * b + 2)
                link(nc.vector.tensor_reduce(ss[:, b].rearrange("p t c -> p (t c)"), sq[:], AX.X, ALU.add))
                link(nc.vector.tensor_scalar(farg[:, b, 0], ss[:, b, :, 0], 1e-24, 1e-24, ALU.max, ALU.mult))
                nc.vector.scalar_tensor_tensor(farg[:, b, 1], farg[:, b, 0], 1e-37, ss[:, b, :, 1],
                                               ALU.max, ALU.max).then_inc(farg_done, 1)

            def self_add(b):
                dve.wait_ge(gelu_done, T * (b + 1))
                xf = xr[:, b].rearrange("p t d -> p (t d)")
                link(nc.vector.tensor_tensor(xf, xf, gz[:, b].rearrange("p t d -> p (t d)"), ALU.add))

            def gating(b):
                dve.wait_ge(logit_mm, b + 1)
                link(nc.vector.scalar_tensor_tensor(logit[:, b], bank[GATE_BANK[b]][:, 0:E], 1.0 / S, row_sb[:, 0:E],
                                                    ALU.mult, ALU.add))
                nc.vector.tensor_reduce(lmax[:, b, 0:1], logit[:, b], AX.X, ALU.max, negate=True).then_inc(logit_done, 1)
                dve.wait_ge(pexp_done, b + 1)
                link(nc.vector.reciprocal(gate[:, b, 0:1], lmax[:, b, 1:2]))
                link(nc.vector.tensor_scalar(prob[:, b], prob[:, b], gate[:, b, 0:1], None, ALU.mult))
                link(nc.vector.max(top[:, b], prob[:, b]))
                link(nc.vector.max_index(top_i[:, b], top[:, b], prob[:, b]))
                nc.vector.tensor_copy(top_f[:, b], top_i[:, b, 0:2])
                link(nc.vector.tensor_tensor(gate[:, b, 1:2], top[:, b, 0:1], top[:, b, 1:2], ALU.add))
                link(nc.vector.reciprocal(gate[:, b, 1:2], gate[:, b, 1:2]))
                link(nc.vector.tensor_scalar(gate[:, b, 2:4], top[:, b, 0:2], gate[:, b, 1:2], a_sb[:, 1:2],
                                             ALU.mult, ALU.mult))
                nc.vector.tensor_copy(coef[:, b, 0:1], a_sb[:, 0:1])
                nc.vector.tensor_scalar(coef[:, b, 1:], iota_f[:], top_f[:, b, 0:1], gate[:, b, 2:3],
                                        ALU.is_equal, ALU.mult)
                link(nc.vector.tensor_scalar(coef2[:, b], iota_f[:], top_f[:, b, 1:2], gate[:, b, 3:4],
                                             ALU.is_equal, ALU.mult))
                nc.vector.tensor_tensor(coef[:, b, 1:], coef[:, b, 1:], coef2[:, b], ALU.add).then_inc(coef_done, 1)
                if b == 0:
                    dve.wait_ge(ld_w1, 32)
                    dve.wait_ge(ld_w2, 32)
                for k in range(2):
                    e = dve.value_load(top_i[0:1, b, k:k + 1], min_val=0, max_val=E - 1)
                    nc.vector.tensor_copy(w1s[:, b, k], w1[:, bass.ds(e * H + H, H)])
                    nc.vector.tensor_scalar(w2s[:, b, k], w2[:, bass.ds(e * H + H, H)], gate[:, b, 2 + k:3 + k], None,
                                            ALU.mult)
                    last = nc.vector.tensor_copy(b1s[:, b, k], rest_sb[:, bass.ds(e * C + REST["b1"][0] + C, C)])
                last.then_inc(chosen, 1)

            for b in range(B):
                layer_norm("cross0", b)
            prep()
            for b in range(B):
                normalise("cross0", b)
            prep_rest()
            for b in range(B):
                softmax_in("cross0", b)
            for b in range(B):
                softmax_out("cross0", b)
            for b in range(B):
                cross_add("cross0", b)
                layer_norm("self", b)
            for b in range(B):
                normalise("self", b)
            for b in range(B):
                split(b)

            for quad in range(QUADS):
                score_max(quad)
                if quad % T == 0 and quad:
                    norm_values(quad // T - 1)
                if quad == PV_LAG + G * T:
                    copy_oT(0)
                if quad == QUADS - 2:
                    dve.wait_ge(ld_w2, 32)
                    nc.vector.tensor_scalar(w2_main[:], w2[:, 0:H], a_sb[:, 0:1], None, ALU.mult).then_inc(prep_done, 1)
            norm_values(B * G - 1)
            copy_oT(1)
            for b in range(B):
                norms(b)
            for b in range(B):
                self_add(b)
                layer_norm("cross1", b)
            for b in range(B):
                normalise("cross1", b)
            for b in range(B):
                softmax_in("cross1", b)
            for b in range(B):
                softmax_out("cross1", b)
            for b in range(B):
                cross_add("cross1", b)
                layer_norm("ffn", b)
            for b in range(B):
                normalise("ffn", b)
            for b in range(B):
                gating(b)
            for b in range(B):
                dve.wait_ge(acc_mm, b + 1)
                nc.vector.tensor_tensor(res[:, b].rearrange("p t d -> p (t d)"), bank[ACC_BANK[b]][:],
                                        xr[:, b].rearrange("p t d -> p (t d)"), ALU.add).then_inc(res_done, 1)

        @block.tensor
        def _(pe):
            def transposes(kind, b):
                dst = bank[T_BANK[kind][b]]
                for t in range(T):
                    pe.wait_ge(xn_done[kind], T * b + t + 1)
                    last = pe.transpose(dst[:, P * t:P * t + P], xn[:, b, t], ident[:])
                last.then_inc(xT_mm[kind], 1)

            def cross_scores(kind, b):
                src, key = (xT, fold) if kind == "cross0" else (keyT, key2)
                if kind == "cross0":
                    pe.wait_ge(xT_done[kind], b + 1)
                    pe.wait_ge(fold_done, 1)
                else:
                    pe.wait_ge(key_done, b + 1)
                for t in range(T):
                    last = pe.matmul(bank[S_BANK[kind][b]][:, KV * t:KV * t + KV], src[:, b, P * t:P * t + P],
                                     key[:, KV * b:KV * b + KV], start=True, stop=True)
                last.then_inc(sc_mm[kind], 1)

            def cross_prT(kind, b):
                pe.wait_ge(pr_done[kind], b + 1)
                pe.transpose(bank[S_BANK[kind][b]][:, P:2 * P], pr[:, b].rearrange("p t k -> p (t k)"),
                             ident[:]).then_inc(prT_mm[kind], 1)

            def cross_av(kind, b):
                pe.wait_ge(prT_done[kind], b + 1)
                pe.matmul(bank[O_BANK[kind][b]][:], prT[:, b], ctx_bd[:, b].rearrange("p t d -> p (t d)"),
                          start=True, stop=True).then_inc(av_mm[kind], 1)

            pe.wait_ge(ld_first, 16)
            pe.matmul(bank[4][:, 0:B * KV], fw("wkT"), fw("ctxT"), start=True, stop=True).then_inc(keys_mm, 1)
            pe.wait_ge(const_done, 1)
            for b in range(B):
                if b == 0:
                    pe.wait_ge(key0_done, 1)
                    pe.matmul(bank[7][:, 0:B * KV], fw("wq0"), key0[:], start=True, stop=True)
                    pe.matmul(bank[7][:, B * KV:2 * B * KV], fw("bq").broadcast_to([P, P]), key0[:],
                              start=True, stop=True).then_inc(fold_mm, 1)
                transposes("cross0", b)
            pe.wait_ge(ld_rest, 16)
            pe.matmul(bank[5][:, 0:B * KV], rw("wxT"), fw("ctxT"), start=True, stop=True).then_inc(key2_mm, 1)
            pe.matmul(bank[6][:, 0:D], rw("woT"), rw("wff"), start=True, stop=True).then_inc(wof_mm, 1)
            for b in range(B):
                cross_scores("cross0", b)
            for b in range(B):
                cross_prT("cross0", b)
            pe.wait_ge(key2_done, 1)
            pe.wait_ge(prep_done, 1)
            pe.wait_ge(ld_ctx, 16 * T)
            for b in range(B):
                cross_av("cross0", b)
            for b in range(B):
                transposes("self", b)
            for b in range(B):
                pe.wait_ge(xT_done["self"], b + 1)
                pe.matmul(bank[Q_BANK[b]][:], rw("wq"), xT[:, b], start=True, stop=True).then_inc(q_mm, 1)
                pe.matmul(bank[K_BANK[b]][:], rw("wk"), xT[:, b], start=True, stop=True).then_inc(k_mm, 1)
                for t in range(T):
                    last = pe.matmul(bank[V_BANK[b]][:, D * t:D * t + D], xT[:, b, P * t:P * t + P], rw("wv"),
                                     start=True, stop=True)
                last.then_inc(v_mm, 1)

            def scores(quad):
                for i in range(J * quad, J * quad + J):
                    b, g, kt, j = tile_of(i)
                    h = J * j + g
                    if i % (G * T * J) == 0:
                        pe.wait_ge(q_stacked[b], 16 * SLOTS)
                        pe.wait_ge(k_stacked[b], 16 * SLOTS)
                        if b == 0:
                            pe.wait_ge(qk_done, 2 * B)
                    if i >= NSC:
                        pe.wait_ge(exp_done, i - NSC + 1)
                    pe.matmul(bank[i % NSC][:], ks[ROWS * b:ROWS * b + ROWS, h, P * kt:P * kt + P],
                              qs[ROWS * b:ROWS * b + ROWS, h],
                              start=True, stop=True).then_inc(score_mm, 1)

            def values(quad):
                b, g, kt, _ = tile_of(J * quad)
                pe.wait_ge(vn_done, quad // T + 1)
                for j in range(J):
                    i = J * quad + j
                    last = pe.matmul(bank[OT_BANK[b]][32 * j:32 * j + 32, :], vn[:, g, J * kt + j], ex[:, i % NE],
                                     start=(g == 0 and kt == 0), stop=(g == G - 1 and kt == T - 1),
                                     skip_group_check=True)
                last.then_inc(pv_done, 1)

            for quad in range(QUADS + PV_LAG):
                if quad < QUADS:
                    scores(quad)
                if quad >= PV_LAG:
                    values(quad - PV_LAG)

            for b in range(B):
                pe.wait_ge(oT_done, b + 1)
                if b == 0:
                    pe.wait_ge(exp_done, QUADS * J)
                for t in range(T):
                    at = (t % 2) * 2 * D
                    last = pe.matmul(bank[Z_BANK[b][t // 2]][:, at:at + 2 * D], oT[:, b, P * t:P * t + P], wof[:],
                                     start=True, stop=True)
                last.then_inc(z_mm, 1)
            for b in range(B):
                transposes("cross1", b)
                pe.wait_ge(xT_done["cross1"], b + 1)
                pe.matmul(bank[KEY_BANK[b]][:], rw("wxT"), xT[:, b], start=True, stop=True).then_inc(key_mm, 1)
            for b in range(B):
                cross_scores("cross1", b)
            for b in range(B):
                cross_prT("cross1", b)
            for b in range(B):
                cross_av("cross1", b)
            for b in range(B):
                transposes("ffn", b)
                pe.wait_ge(xT_done["ffn"], b + 1)
                pe.matmul(bank[GATE_BANK[b]][:, 0:E], xsum[:, b:b + 1].broadcast_to([P, P]), rw("wg"),
                          start=True, stop=True).then_inc(logit_mm, 1)
                pe.wait_ge(coef_done, b + 1)
                pe.matmul(bank[GATE_BANK[b]][0:E + 1, P:2 * P], coef[:, b], ident[:, 0:1].broadcast_to([P, P]),
                          start=True, stop=True).then_inc(coefT_mm, 1)
            pe.wait_ge(prep_done, 2)
            UN = B * NETS * C

            def hidden(u):
                b, net, c = u // (NETS * C), u // C % NETS, u % C
                if c == 0 and net == 1:
                    pe.wait_ge(chosen, b + 1)
                if c == 0 and net == 0:
                    pe.wait_ge(coefT_done, b + 1)
                if u >= 2:
                    pe.wait_ge(hid_done, u - 1)
                w = w1[:, P * c:P * c + P] if net == 0 else w1s[:, b, net - 1, P * c:P * c + P]
                pe.matmul(bank[H_BANK[b][u % 2]][:], w, x3T[:, b], start=True, stop=True).then_inc(hid_mm, 1)

            def project(u):
                b, net, c = u // (NETS * C), u // C % NETS, u % C
                acc = bank[ACC_BANK[b]]
                pe.wait_ge(hid_done, u + 1)
                w = w2_main if net == 0 else w2s[:, b, net - 1]
                for t in range(T):
                    last = pe.matmul(acc[:, D * t:D * t + D], hid[:, u % 4, P * t:P * t + P],
                                     w[:, D * c:D * c + D], start=(net == 0 and c == 0 and t == 0), stop=False,
                                     skip_group_check=True)
                last.then_inc(hid_used, 1)
                if net == NETS - 1 and c == C - 1:
                    if b == 0:
                        pe.wait_ge(ld_b2, 16)
                    for t in range(T):
                        last = pe.matmul(acc[:, D * t:D * t + D], coefT[:, b], b2_sb[:], start=False, stop=(t == T - 1),
                                         skip_group_check=True)
                    last.then_inc(acc_mm, 1)

            hidden(0)
            for u in range(UN):
                if u + 1 < UN:
                    hidden(u + 1)
                project(u)


def kernel(**inputs):
    import numpy as np
    import concourse.bacc as bacc
    from concourse.bass_utils import run_bass_kernel_spmd

    a = {k: np.asarray(val) for k, val in inputs.items()}
    col = lambda n: a[n].reshape(-1, 1)
    by_row = lambda w: w.reshape(D, HEADS, DH).transpose(0, 2, 1).reshape(D, D)
    b1 = np.concatenate([a["L1_ffn_b1m"].reshape(1, H), a["L1_ffn_b1e"]]).reshape(E + 1, C, P)
    mask = np.zeros((B * KV, 4), np.uint8)
    mask[:, 0] = a["mask_BxS2_bf0"].reshape(B * KV).view(np.uint8)
    host = dict(
        x=a["x"],
        ctx=a["ctx_1024"],
        first=np.concatenate([a["L0_xattn_Wk"].T, a["L0_xattn_Wq"], a["ctx_1024"].reshape(B * KV, D).T,
                              col("L0_xattn_bk"), col("L0_xattn_bq")], axis=1),
        rest=np.concatenate([by_row(a["L0_ffn_Wq"]), by_row(a["L0_ffn_Wk"]), a["L0_ffn_Wv"], a["L0_ffn_Wo"], a["L0_ffn_Wo"].T,
                             a["L0_ffn_Wff"], a["L1_xattn_W"].T, a["L1_ffn_w_gate"], col("L1_xattn_b"),
                             col("L1_xattn_D"), b1.transpose(2, 0, 1).reshape(P, (E + 1) * C)], axis=1),
        w1m=a["L1_ffn_W1m"],
        w1e=a["L1_ffn_W1e"],
        w2m=a["L1_ffn_W2m"],
        w2e=a["L1_ffn_W2e"],
        b2=np.concatenate([a["L1_ffn_b2m"].reshape(1, D), a["L1_ffn_b2e"]]),
        row=np.concatenate([a["L1_ffn_b_gate"].reshape(1, E), a["L1_ffn_alpha"].reshape(1, 1)], axis=1),
        mask=mask.reshape(1, 4 * B * KV).view(np.int32),
    )
    nc = bacc.Bacc("TRN2", target_bir_lowering=False, num_devices=1)
    arrays, args = {}, []
    for name, arr in host.items():
        arr = np.ascontiguousarray(arr)
        arrays[f"in_{name}"] = arr
        args.append(nc.dram_tensor(f"in_{name}", arr.shape, mybir.dt.from_np(arr.dtype), kind="ExternalInput").ap())
    args.append(nc.dram_tensor("out_0", (B, S, D), F32, kind="ExternalOutput").ap())
    block_kernel(nc, *args)
    r = run_bass_kernel_spmd(nc, [arrays], core_ids=[0])
    return r.results[0]["out_0"]
```

```python
from contextlib import ExitStack

import concourse.bass as bass
from concourse import mybir

ALU = mybir.AluOpType
ACT = mybir.ActivationFunctionType
F32 = mybir.dt.float32
BF16 = mybir.dt.bfloat16
U32 = mybir.dt.uint32
AX = mybir.AxisListType

P = 128
B, S, D = 2, 512, 128
T = S // P
KV = 32
HEADS, DH = 16, 8
G, J = 4, 4
E, H, C = 8, 512, 4
NETS = 3
LN_EPS = 1e-5
PARTS = 3
SLOTS = PARTS * PARTS - 1
ROWS = SLOTS * DH
PAIRS = [(0, 0), (0, 1), (1, 0), (1, 1), (0, 2), (1, 2), (2, 0), (2, 1)]
QK_SCALE = (-float(D) ** -0.5, 1.0)
SCORE_BANK = (0, 1, 2, 3, 7)
NSC = len(SCORE_BANK)
NE = 16
QUADS = B * G * T
PV_LAG = 2

WARM = (3, 2, 2, 6, 0, 8, 20)

WARM_TILES = 3

FIRST = dict(wkT=(0, 128), wq0=(128, 128), ctxT=(256, 64), bk=(320, 1), bq=(321, 1))
FIRST_N = 322
REST = dict(wq=(0, 128), wk=(128, 128), wv=(256, 128), wo=(384, 128), woT=(512, 128), wff=(640, 128),
            wxT=(768, 128), wg=(896, E), bx=(904, 1), dx=(905, 1), b1=(906, (E + 1) * C))
REST_N = 906 + (E + 1) * C


def block_kernel(nc, x, xt, ctx, first, rest, w1m, w1e, w2m, w2e, b2, row, mask, out):
    with ExitStack() as stack:
        def sb(name, shape, dt=F32):
            return stack.enter_context(nc.sbuf_tensor(name, shape, dt))

        def sem(name):
            return stack.enter_context(nc.semaphore(name))

        bank = [stack.enter_context(nc.psum_tensor(f"bank{i}", [P, 512], F32)) for i in range(8)]

        ident = sb("ident", [P, P])
        minus_half = sb("minus_half", [P, T])
        minus_one = sb("minus_one", [P, J])
        iota_u = sb("iota_u", [P, E], mybir.dt.int32)
        iota_f = sb("iota_f", [P, E])
        first_sb = sb("first_sb", [P, FIRST_N])
        rest_sb = sb("rest_sb", [P, REST_N])
        ctx_bd = sb("ctx_bd", [P, B, T, D])
        w1 = sb("w1", [P, (E + 1) * H])
        w2 = sb("w2", [P, (E + 1) * H])
        b2_sb = sb("b2_sb", [E + 1, D])
        row_sb = sb("row_sb", [P, E + 1])
        mask_sb = sb("mask_sb", [P, B * KV], mybir.dt.int32)
        mask_bias = sb("mask_bias", [P, B * KV])
        a_sb = sb("a_sb", [P, 2])
        bk_scaled = sb("bk_scaled", [P, 1])
        wq0m = sb("wq0m", [P, 1])
        wq0c = sb("wq0c", [P, D])
        warm_src = sb("warm_src", [P, S], BF16)
        w2_main = sb("w2_main", [P, H])
        wof = sb("wof", [P, 2 * D])
        key0 = sb("key0", [P, B * KV])
        fold = sb("fold", [P, 2 * B * KV])
        key2 = sb("key2", [P, B * KV])

        def fw(name):
            at, n = FIRST[name]
            return first_sb[:, at:at + n]

        def rw(name):
            at, n = REST[name]
            return rest_sb[:, at:at + n]

        xr = sb("xr", [P, B, T, D])
        xn = sb("xn", [P, B, T, D])
        xT = sb("xT", [P, B, S])
        x3T = xn[:].rearrange("p b t d -> p b (t d)")
        stats = sb("stats", [P, B, T, 6])
        mv = sb("mv", [P, B, T, 2])
        veps = sb("veps", [P, B, T])
        rstd = sb("rstd", [P, B, T])
        sm = sb("sm", [P, B, T, KV])
        smx = sb("smx", [P, B, T])
        pr = sb("pr", [P, B, T, KV])
        prT = sb("prT", [P, B, P])
        keyT = sb("keyT", [P, B, S])
        early = sb("early", [P, 2, B, 2, S])
        left = early[:, 0]
        w1s, w2s = early[:, 0], early[:, 1]
        parts = sb("parts", [P, B * 2 * PARTS * S], BF16)
        qkp = parts[:].rearrange("p (b c s) -> p b c s", b=B, c=2 * PARTS)
        hid = parts[:, 0:4 * 2 * S].bitcast(F32).rearrange("p (u s) -> p u s", u=4)
        qks = sb("qks", [B * ROWS, HEADS, 2, S], BF16)
        v = sb("v", [P, B, T, J, KV])
        vn = sb("vn", [P, G, T * J, KV])
        ex = sb("ex", [P, NE, S])
        neg_max = sb("neg_max", [P, QUADS * J])
        sums = sb("sums", [P, QUADS * J])
        rsum = sb("rsum", [P, QUADS * J])
        oT = parts[:, 4 * 2 * S:].bitcast(F32).rearrange("p (b s) -> p b s", b=B)
        sq = early[:, 1].rearrange("p b w (a d) -> p b (w a) d", d=D)
        ss = sb("ss", [P, B, T, 2])
        farg = sb("farg", [P, B, 2, T])
        fz = sb("fz", [P, B, T])
        gz = early[:, 0].rearrange("p b w (a d) -> p b (w a) d", d=D)[:, :, 0:T]
        xsum = sb("xsum", [P, B])
        logit = sb("logit", [P, B, E])
        lmax = sb("lmax", [P, B, 2])
        prob = sb("prob", [P, B, E])
        top = sb("top", [P, B, 8])
        top_i = sb("top_i", [P, B, 8], U32)
        top_f = sb("top_f", [P, B, 2])
        gate = sb("gate", [P, B, 4])
        coef = sb("coef", [P, B, E + 1])
        coef2 = sb("coef2", [P, B, E])
        coefT = sb("coefT", [E + 1, B, P])
        b1s = sb("b1s", [P, B, 2, C])
        res = xT[:].rearrange("p b (t d) -> p b t d", t=T)

        ld_first, ld_rest, ld_small = sem("ld_first"), sem("ld_rest"), sem("ld_small")
        ld_ctx, ld_w1, ld_w2, ld_b2 = sem("ld_ctx"), sem("ld_w1"), sem("ld_w2"), sem("ld_b2")
        ld_x = [sem(f"ld_x{b}") for b in range(B)]
        ld_xT = [sem(f"ld_xT{b}") for b in range(B)]
        rsum_done = sem("rsum_done")
        warm_zero, wq0c_done, main_scaled = sem("warm_zero"), sem("wq0c_done"), sem("main_scaled")
        st_out = sem("st_out")
        const_done = sem("const_done")
        bd_zero = sem("bd_zero")
        pool_step = sem("pool_step")
        v_step = sem("v_step")
        a_step = sem("a_step")
        keys_mm, key0_done, fold_mm, fold_done, key2_mm, key2_done, wof_mm, prep_done = (
            sem(n) for n in ("keys_mm", "key0_done", "fold_mm", "fold_done", "key2_mm", "key2_done",
                             "wof_mm", "prep_done"))
        KINDS = ("cross0", "self", "cross1", "ffn")
        var_done = {k: sem(f"var_{k}") for k in KINDS}
        rstd_done = {k: sem(f"rstd_{k}") for k in KINDS}
        xn_done = {k: sem(f"xn_{k}") for k in KINDS}
        xT_mm = {k: sem(f"xT_mm_{k}") for k in KINDS}
        xT_done = {k: sem(f"xT_{k}") for k in KINDS}
        CROSS = ("cross0", "cross1")
        sc_mm = {k: sem(f"sc_mm_{k}") for k in CROSS}
        shifted = {k: sem(f"shifted_{k}") for k in CROSS}
        expd = {k: sem(f"expd_{k}") for k in CROSS}
        pr_done = {k: sem(f"pr_{k}") for k in CROSS}
        prT_mm = {k: sem(f"prT_mm_{k}") for k in CROSS}
        prT_done = {k: sem(f"prT_{k}") for k in CROSS}
        av_mm = {k: sem(f"av_mm_{k}") for k in CROSS}
        x_done = {k: sem(f"x_{k}") for k in CROSS}
        key_mm, key_done = sem("key_mm"), sem("key_done")
        q_mm, k_mm, v_mm = sem("q_mm"), sem("k_mm"), sem("v_mm")
        p1_done, r1_done, p2_done, p3_done = (sem(n) for n in ("p1_done", "r1_done", "p2_done", "p3_done"))
        v_done = sem("v_done")
        stacked = [sem(f"stacked{b}") for b in range(B)]
        score_mm, max_done, exp_done, vn_done, pv_done = (
            sem(n) for n in ("score_mm", "max_done", "exp_done", "vn_done", "pv_done"))
        oT_done, z_mm, sq_done, farg_done, fz_done, gelu_done = (
            sem(n) for n in ("oT_done", "z_mm", "sq_done", "farg_done", "fz_done", "gelu_done"))
        logit_mm, logit_done, pexp_done, coef_done, coefT_mm, coefT_done, chosen = (
            sem(n) for n in ("logit_mm", "logit_done", "pexp_done", "coef_done", "coefT_mm",
                             "coefT_done", "chosen"))
        hid_mm, hid_done, hid_used, res_done = (sem(n) for n in ("hid_mm", "hid_done", "hid_used", "res_done"))

        T_BANK = {"self": (0, 3), "cross1": (4, 5), "ffn": (4, 5)}
        S_BANK = {"cross0": (1, 4), "cross1": (4, 1)}
        O_BANK = {"cross0": (2, 5), "cross1": (6, 0)}
        Q_BANK, K_BANK, V_BANK = (1, 4), (2, 5), (6, 7)
        OT_BANK = (4, 5)
        Z_BANK = ((4, 6), (0, 1))
        KEY_BANK = (6, 0)
        GATE_BANK = (6, 1)
        H_BANK = (2, 3, 7)
        ACC_BANK = (4, 5)
        WARM_BANK = 3

        def tile_of(i):
            return i // (G * T * J), i // (T * J) % G, i // J % T, i % J

        block = stack.enter_context(nc.Block())

        @block.sync
        def _(sp):
            sp.dma_start(first_sb[:], first).then_inc(ld_first, 16)
            for b in range(B):
                sp.dma_start(xr[:, b], x[b].rearrange("(t p) d -> p t d", p=P)).then_inc(ld_x[b], 16)
                sp.dma_start(xT[:, b], xt[:, b]).then_inc(ld_xT[b], 16)
            sp.wait_ge(bd_zero, 1)
            for t in range(T):
                sp.dma_start(ctx_bd[KV * t:KV * t + KV, :, t, :],
                             ctx.rearrange("b k d -> k b d")).then_inc(ld_ctx, 16)
            sp.dma_start(rest_sb[:], rest).then_inc(ld_rest, 16)
            sp.dma_start(row_sb[:], row.broadcast_to([P, E + 1])).then_inc(ld_small, 16)
            sp.dma_start(mask_sb[:], mask.broadcast_to([P, B * KV])).then_inc(ld_small, 16)
            sp.dma_start(b2_sb[:], b2).then_inc(ld_b2, 16)
            part_done = (p1_done, p2_done, p3_done)
            for b in range(B):
                for n, (cq, ck) in enumerate(PAIRS):
                    sp.wait_ge(part_done[max(cq, ck)], 2 * b + 2)
                    step = PARTS + ck - cq
                    r = ROWS * b + DH * n
                    sp.dma_start(qks[r:r + DH], qkp[:, b, cq:PARTS + ck + 1:step]).then_inc(stacked[b], 16)
            sp.dma_start(w1[:, 0:H], w1m).then_inc(ld_w1, 16)
            sp.dma_start(w1[:, H:].rearrange("d (e h) -> d e h", e=E),
                         w1e.rearrange("e d h -> d e h")).then_inc(ld_w1, 16)
            sp.dma_start(w2[:, 0:H].rearrange("p (c d) -> p c d", c=C),
                         w2m.rearrange("(c p) d -> p c d", p=P)).then_inc(ld_w2, 16)
            sp.dma_start(w2[:, H:].rearrange("p (e d) -> p e d", e=E * C),
                         w2e.rearrange("e (c p) d -> p (e c) d", p=P)).then_inc(ld_w2, 16)
            for b in range(B):
                sp.wait_ge(res_done, b + 1)
                sp.dma_start(out[b].rearrange("(t p) d -> p t d", p=P), res[:, b]).then_inc(st_out, 16)
            sp.wait_ge(st_out, 16 * B)

        @block.gpsimd
        def _(pool):
            nc.gpsimd.memset(warm_src[:], 0.0).then_inc(warm_zero, 1)
            nc.gpsimd.memset(minus_half[:], -0.5)
            nc.gpsimd.memset(minus_one[:], -1.0)
            nc.gpsimd.memset(ident[:], 0.0).then_inc(pool_step, 1)
            nc.gpsimd.memset(ctx_bd[:], 0.0).then_inc(bd_zero, 1)
            pool.wait_ge(pool_step, 1)
            nc.gpsimd.affine_select(out=ident[:], in_=ident[:], compare_op=ALU.not_equal, fill=1.0, base=0,
                                    pattern=[[-1, P]], channel_multiplier=1).then_inc(const_done, 1)
            nc.gpsimd.iota(iota_u[:], pattern=[[1, E]], base=0, channel_multiplier=0).then_inc(const_done, 1)

            def rstd_of(kind, b):
                pool.wait_ge(var_done[kind], b + 1)
                nc.gpsimd.tensor_tensor(rstd[:, b], veps[:, b], minus_half[:], ALU.pow).then_inc(rstd_done[kind], 1)

            rstd_of("cross0", 0)
            rstd_of("cross0", 1)
            nc.gpsimd.memset(vn[:], 0.0).then_inc(const_done, 1)
            rstd_of("self", 0)
            rstd_of("self", 1)

            def norm_values(quad):
                b, g, kt, _ = tile_of(J * quad)
                if quad == 0:
                    pool.wait_ge(v_done, B)
                    pool.wait_ge(const_done, 3)
                if b:
                    pool.wait_ge(pv_done, quad - G * T + 1)
                a, z = J * quad, J * quad + J
                pool.wait_ge(exp_done, z)
                nc.gpsimd.tensor_tensor(rsum[:, a:z], sums[:, a:z], minus_one[:], ALU.pow).then_inc(rsum_done, 1)
                pool.wait_ge(rsum_done, quad + 1)
                nc.gpsimd.tensor_tensor(vn[:, g, J * kt:J * kt + J, DH * g:DH * g + DH],
                                        v[:, b, kt, :, DH * g:DH * g + DH],
                                        rsum[:, a:z].unsqueeze(2).broadcast_to([P, J, DH]),
                                        ALU.mult).then_inc(vn_done, 1)

            def norm_z(b):
                pool.wait_ge(farg_done, b + 1)
                nc.gpsimd.tensor_tensor(fz[:, b], farg[:, b, 1], minus_half[:], ALU.pow).then_inc(fz_done, 1)

            for quad in range(QUADS):
                norm_values(quad)
                if quad == 18:
                    norm_z(0)
                if quad == 20:
                    rstd_of("cross1", 0)
                if quad == 27:
                    rstd_of("ffn", 0)
            norm_z(1)
            rstd_of("cross1", 1)
            rstd_of("ffn", 1)

        @block.scalar
        def _(act):
            def copy_xT(kind, b):
                act.wait_ge(xT_mm[kind], b + 1)
                src = bank[T_BANK[kind][b]][:]
                if kind == "ffn":
                    nc.scalar.activation(x3T[:, b], src, ACT.Copy,
                                         accum_out=xsum[:, b:b + 1]).then_inc(xT_done[kind], 1)
                else:
                    nc.scalar.activation(xT[:, b], src, ACT.Copy).then_inc(xT_done[kind], 1)

            def cross_exp(kind, b):
                act.wait_ge(shifted[kind], b + 1)
                nc.scalar.activation(pr[:, b], sm[:, b], ACT.Exp).then_inc(expd[kind], 1)

            def cross_prT(kind, b):
                act.wait_ge(prT_mm[kind], b + 1)
                nc.scalar.activation(prT[:, b], bank[S_BANK[kind][b]][:, P:2 * P], ACT.Copy).then_inc(prT_done[kind], 1)

            def split(b):
                for which, ready, src in ((0, q_mm, Q_BANK), (1, k_mm, K_BANK)):
                    act.wait_ge(ready, b + 1)
                    nc.scalar.activation(qkp[:, b, PARTS * which], bank[src[b]][:], ACT.Copy,
                                         scale=QK_SCALE[which]).then_inc(p1_done, 1)

            def split_rest(b):
                for which in range(2):
                    act.wait_ge(r1_done, 2 * b + which + 1)
                    nc.scalar.activation(qkp[:, b, PARTS * which + 1], left[:, b, which], ACT.Copy).then_inc(p2_done, 1)

            def exps(quad):
                for i in range(J * quad, J * quad + J):
                    act.wait_ge(max_done, i + 1)
                    if i >= NE:
                        act.wait_ge(pv_done, (i - NE) // J + 1)
                    nc.scalar.activation(ex[:, i % NE], bank[SCORE_BANK[i % NSC]][:], ACT.Exp, bias=neg_max[:, i:i + 1],
                                         scale=-1.0, accum_out=sums[:, i:i + 1]).then_inc(exp_done, 1)

            def squares(b):
                act.wait_ge(z_mm, b + 1)
                for half in range(2):
                    nc.scalar.activation(sq[:, b, 4 * half:4 * half + 4].rearrange("p a d -> p (a d)"),
                                         bank[Z_BANK[b][half]][:], ACT.Square).then_inc(sq_done, 1)

            def gelu_z(b):
                act.wait_ge(fz_done, b + 1)
                for t in range(T):
                    at = (t % 2) * 2 * D + D
                    nc.scalar.activation(gz[:, b, t], bank[Z_BANK[b][t // 2]][:, at:at + D], ACT.Gelu,
                                         scale=fz[:, b, t:t + 1]).then_inc(gelu_done, 1)

            def relu_key(b):
                act.wait_ge(key_mm, b + 1)
                nc.scalar.activation(keyT[:, b], bank[KEY_BANK[b]][:], ACT.Relu, bias=rw("bx")).then_inc(key_done, 1)

            def gate_exp(b):
                act.wait_ge(logit_done, b + 1)
                nc.scalar.activation(prob[:, b], logit[:, b], ACT.Exp, bias=lmax[:, b, 0:1],
                                     accum_out=lmax[:, b, 1:2]).then_inc(pexp_done, 1)

            def copy_coefT(b):
                act.wait_ge(coefT_mm, b + 1)
                nc.scalar.activation(coefT[:, b], bank[GATE_BANK[b]][0:E + 1, P:2 * P], ACT.Copy).then_inc(coefT_done, 1)

            def hidden_gelu(u):
                b, net, c = u // (NETS * C), u // C % NETS, u % C
                act.wait_ge(hid_mm, u + 1)
                if u >= 4:
                    act.wait_ge(hid_used, u - 3)
                if net == 0:
                    bias = rw("b1")[:, c:c + 1]
                else:
                    act.wait_ge(chosen, b + 1)
                    bias = b1s[:, b, net - 1, c:c + 1]
                nc.scalar.activation(hid[:, u % 4], bank[H_BANK[u % 3]][:], ACT.Gelu_apprx_tanh,
                                     bias=bias).then_inc(hid_done, 1)

            act.wait_ge(ld_first, 16)
            nc.scalar.activation(bk_scaled[:], fw("bk"), ACT.Copy, scale=1.0 / 32.0).then_inc(a_step, 1)
            act.wait_ge(a_step, 1)
            act.wait_ge(keys_mm, 1)
            nc.scalar.activation(key0[:], bank[0][:, 0:B * KV], ACT.Identity, bias=bk_scaled[:, 0:1],
                                 scale=1.0 / 32.0).then_inc(key0_done, 1)
            act.wait_ge(fold_mm, 1)
            nc.scalar.activation(fold[:], bank[7][:, 0:2 * B * KV], ACT.Copy).then_inc(fold_done, 1)
            for b in range(B):
                cross_exp("cross0", b)
            for b in range(B):
                cross_prT("cross0", b)
            copy_xT("self", 0)
            split(0)
            copy_xT("self", 1)
            split_rest(0)
            split(1)
            split_rest(1)
            for b in range(B):
                act.wait_ge(v_mm, b + 1)
                nc.scalar.activation(v[:, b].rearrange("p t j c -> p (t j c)"), bank[V_BANK[b]][:], ACT.Copy).then_inc(v_done, 1)

            for quad in range(QUADS):
                exps(quad)
                if quad == 18:
                    squares(0)
                if quad == 19:
                    gelu_z(0)
                if quad == 22:
                    copy_xT("cross1", 0)
                if quad == 24:
                    relu_key(0)
                if quad == 25:
                    cross_exp("cross1", 0)
                if quad == 27:
                    cross_prT("cross1", 0)
                if quad == 30:
                    copy_xT("ffn", 0)
            gate_exp(0)
            hidden_gelu(0)
            act.wait_ge(pv_done, B * G * T)
            nc.scalar.activation(oT[:, 1], bank[OT_BANK[1]][:], ACT.Copy).then_inc(oT_done, 1)
            squares(1)
            hidden_gelu(1)
            gelu_z(1)
            copy_coefT(0)
            for u in range(2, B * NETS * C):
                hidden_gelu(u)
                if u == 4:
                    copy_xT("cross1", 1)
                if u == 5:
                    relu_key(1)
                if u == 6:
                    cross_exp("cross1", 1)
                if u == 7:
                    cross_prT("cross1", 1)
                if u == 10:
                    copy_xT("ffn", 1)
                    gate_exp(1)
                if u == 14:
                    copy_coefT(1)

        @block.vector
        def _(dve):
            links = [0]

            def link(ins):
                links[0] += 1
                ins.then_inc(v_step, 1)
                dve.wait_ge(v_step, links[0])

            def layer_norm(kind, b):
                if kind == "cross0":
                    dve.wait_ge(ld_x[b], 16)
                for t in range(T):
                    last = nc.vector.bn_stats(stats[:, b, t], xr[:, b, t])
                link(last)
                for t in range(T):
                    last = nc.vector.bn_aggr(mv[:, b, t], stats[:, b, t])
                link(last)
                nc.vector.tensor_scalar(veps[:, b], mv[:, b, :, 1], LN_EPS, None, ALU.add).then_inc(var_done[kind], 1)

            def normalise(kind, b):
                dve.wait_ge(rstd_done[kind], b + 1)
                for t in range(T):
                    nc.vector.tensor_scalar(xn[:, b, t], xr[:, b, t], mv[:, b, t, 0:1], rstd[:, b, t:t + 1],
                                            ALU.subtract, ALU.mult).then_inc(xn_done[kind], 1)

            def softmax_in(kind, b):
                if kind == "cross0" and b == 0:
                    dve.wait_ge(fold_done, 1)
                bias = fold[:, B * KV + KV * b:B * KV + KV * b + KV] if kind == "cross0" else mask_bias[:, KV * b:KV * b + KV]
                dve.wait_ge(sc_mm[kind], b + 1)
                ps = bank[S_BANK[kind][b]][:, 0:T * KV].rearrange("p (t k) -> p t k", t=T)
                if kind == "cross0":
                    dve.wait_ge(rstd_done[kind], b + 1)
                    link(nc.vector.tensor_tensor(sm[:, b], ps, rstd[:, b].unsqueeze(2).broadcast_to([P, T, KV]), ALU.mult))
                    ps = sm[:, b]
                link(nc.vector.tensor_tensor(sm[:, b], ps, bias.unsqueeze(1).broadcast_to([P, T, KV]), ALU.add))
                link(nc.vector.tensor_reduce(smx[:, b], sm[:, b], AX.X, ALU.max))
                nc.vector.tensor_tensor(sm[:, b], sm[:, b], smx[:, b].unsqueeze(2).broadcast_to([P, T, KV]),
                                        ALU.subtract).then_inc(shifted[kind], 1)

            def softmax_out(kind, b):
                dve.wait_ge(expd[kind], b + 1)
                link(nc.vector.tensor_reduce(smx[:, b], pr[:, b], AX.X, ALU.add))
                link(nc.vector.reciprocal(smx[:, b], smx[:, b]))
                nc.vector.tensor_tensor(pr[:, b], pr[:, b], smx[:, b].unsqueeze(2).broadcast_to([P, T, KV]),
                                        ALU.mult).then_inc(pr_done[kind], 1)

            def cross_add(kind, b):
                dve.wait_ge(av_mm[kind], b + 1)
                xf = xr[:, b].rearrange("p t d -> p (t d)")
                nc.vector.tensor_tensor(xf, bank[O_BANK[kind][b]][:], xf, ALU.add).then_inc(x_done[kind], 1)
                dve.wait_ge(x_done[kind], b + 1)

            def centre_wq0():
                dve.wait_ge(ld_first, 16)
                link(nc.vector.tensor_reduce(wq0m[:], fw("wq0"), AX.X, ALU.add))
                link(nc.vector.tensor_scalar(wq0m[:], wq0m[:], 1.0 / D, None, ALU.mult))
                nc.vector.tensor_scalar(wq0c[:], fw("wq0"), wq0m[:, 0:1], None, ALU.subtract).then_inc(wq0c_done, 1)

            def prep_rest():
                dve.wait_ge(ld_rest, 16)
                dve.wait_ge(key2_mm, 1)
                link(nc.vector.tensor_scalar(key2[:], bank[5][:, 0:B * KV], rw("bx"), 0.0, ALU.add, ALU.max))
                nc.vector.tensor_scalar(key2[:], key2[:], rw("dx"), None, ALU.mult).then_inc(key2_done, 1)
                nc.vector.tensor_copy(wof[:, 0:D], rw("wo"))
                dve.wait_ge(wof_mm, 1)
                nc.vector.tensor_copy(wof[:, D:], bank[6][:, 0:D]).then_inc(prep_done, 1)
                dve.wait_ge(ld_small, 32)
                nc.vector.tensor_scalar(mask_bias[:], mask_sb[:], -1e30, None, ALU.mult)
                link(nc.vector.tensor_scalar(a_sb[:, 0:1], row_sb[:, E:E + 1], 0.1, 1.0, ALU.max, ALU.min))
                nc.vector.tensor_scalar(a_sb[:, 1:2], a_sb[:, 0:1], -1.0, 1.0, ALU.mult, ALU.add)
                dve.wait_ge(const_done, 3)
                link(nc.vector.tensor_copy(iota_f[:], iota_u[:]))

            def split(b):
                for which, src in ((0, Q_BANK), (1, K_BANK)):
                    dve.wait_ge(p1_done, 2 * b + which + 1)
                    nc.vector.scalar_tensor_tensor(left[:, b, which], bank[src[b]][:], QK_SCALE[which],
                                                   qkp[:, b, PARTS * which], ALU.mult, ALU.subtract).then_inc(r1_done, 1)
                for which in range(2):
                    dve.wait_ge(p2_done, 2 * b + which + 1)
                    nc.vector.tensor_tensor(qkp[:, b, PARTS * which + 2], left[:, b, which],
                                            qkp[:, b, PARTS * which + 1], ALU.subtract).then_inc(p3_done, 1)

            def score_max(quad):
                for i in range(J * quad, J * quad + J):
                    dve.wait_ge(score_mm, i + 1)
                    nc.vector.tensor_reduce(neg_max[:, i:i + 1], bank[SCORE_BANK[i % NSC]][:], AX.X, ALU.min).then_inc(max_done, 1)

            def norms(b):
                dve.wait_ge(sq_done, 2 * b + 2)
                link(nc.vector.tensor_reduce(ss[:, b].rearrange("p t c -> p (t c)"), sq[:, b], AX.X, ALU.add))
                link(nc.vector.tensor_scalar(farg[:, b, 0], ss[:, b, :, 0], 1e-24, 1e-24, ALU.max, ALU.mult))
                nc.vector.scalar_tensor_tensor(farg[:, b, 1], farg[:, b, 0], 1e-37, ss[:, b, :, 1],
                                               ALU.max, ALU.max).then_inc(farg_done, 1)

            def self_add(b):
                dve.wait_ge(gelu_done, T * (b + 1))
                xf = xr[:, b].rearrange("p t d -> p (t d)")
                link(nc.vector.tensor_tensor(xf, xf, gz[:, b].rearrange("p t d -> p (t d)"), ALU.add))

            def gating(b):
                dve.wait_ge(logit_mm, b + 1)
                link(nc.vector.scalar_tensor_tensor(logit[:, b], bank[GATE_BANK[b]][:, 0:E], 1.0 / S, row_sb[:, 0:E],
                                                    ALU.mult, ALU.add))
                nc.vector.tensor_reduce(lmax[:, b, 0:1], logit[:, b], AX.X, ALU.max, negate=True).then_inc(logit_done, 1)
                dve.wait_ge(pexp_done, b + 1)
                link(nc.vector.reciprocal(gate[:, b, 0:1], lmax[:, b, 1:2]))
                link(nc.vector.tensor_scalar(prob[:, b], prob[:, b], gate[:, b, 0:1], None, ALU.mult))
                link(nc.vector.max(top[:, b], prob[:, b]))
                link(nc.vector.max_index(top_i[:, b], top[:, b], prob[:, b]))
                nc.vector.tensor_copy(top_f[:, b], top_i[:, b, 0:2])
                link(nc.vector.tensor_tensor(gate[:, b, 1:2], top[:, b, 0:1], top[:, b, 1:2], ALU.add))
                link(nc.vector.reciprocal(gate[:, b, 1:2], gate[:, b, 1:2]))
                link(nc.vector.tensor_scalar(gate[:, b, 2:4], top[:, b, 0:2], gate[:, b, 1:2], a_sb[:, 1:2],
                                             ALU.mult, ALU.mult))
                nc.vector.tensor_copy(coef[:, b, 0:1], a_sb[:, 0:1])
                nc.vector.tensor_scalar(coef[:, b, 1:], iota_f[:], top_f[:, b, 0:1], gate[:, b, 2:3],
                                        ALU.is_equal, ALU.mult)
                link(nc.vector.tensor_scalar(coef2[:, b], iota_f[:], top_f[:, b, 1:2], gate[:, b, 3:4],
                                             ALU.is_equal, ALU.mult))
                nc.vector.tensor_tensor(coef[:, b, 1:], coef[:, b, 1:], coef2[:, b], ALU.add).then_inc(coef_done, 1)
                if b == 0:
                    dve.wait_ge(ld_w1, 32)
                    dve.wait_ge(ld_w2, 32)
                for k in range(2):
                    e = dve.value_load(top_i[0:1, b, k:k + 1], min_val=0, max_val=E - 1)
                    nc.vector.tensor_copy(w1s[:, b, k], w1[:, bass.ds(e * H + H, H)])
                    nc.vector.tensor_scalar(w2s[:, b, k], w2[:, bass.ds(e * H + H, H)], gate[:, b, 2 + k:3 + k], None,
                                            ALU.mult)
                    last = nc.vector.tensor_copy(b1s[:, b, k], rest_sb[:, bass.ds(e * C + REST["b1"][0] + C, C)])
                last.then_inc(chosen, 1)

            def result(b):
                dve.wait_ge(hid_used, (b + 1) * NETS * C)
                nc.vector.tensor_tensor(res[:, b].rearrange("p t d -> p (t d)"), bank[ACC_BANK[b]][:],
                                        xr[:, b].rearrange("p t d -> p (t d)"), ALU.add).then_inc(res_done, 1)

            centre_wq0()
            for b in range(B):
                layer_norm("cross0", b)
            for b in range(B):
                softmax_in("cross0", b)
            for b in range(B):
                softmax_out("cross0", b)
            prep_rest()
            cross_add("cross0", 0)
            layer_norm("self", 0)
            cross_add("cross0", 1)
            normalise("self", 0)
            layer_norm("self", 1)
            normalise("self", 1)
            for b in range(B):
                split(b)

            for quad in range(QUADS):
                score_max(quad)
                if quad == 12:
                    dve.wait_ge(ld_w2, 32)
                    nc.vector.tensor_scalar(w2_main[:], w2[:, 0:H], a_sb[:, 0:1], None, ALU.mult).then_inc(main_scaled, 1)
                if quad == 17:
                    dve.wait_ge(pv_done, G * T)
                    nc.vector.tensor_copy(oT[:, 0], bank[OT_BANK[0]][:]).then_inc(oT_done, 1)
                if quad == 19:
                    norms(0)
                if quad == 21:
                    self_add(0)
                    layer_norm("cross1", 0)
                if quad == 22:
                    normalise("cross1", 0)
                if quad == 25:
                    softmax_in("cross1", 0)
                if quad == 26:
                    softmax_out("cross1", 0)
                if quad == 28:
                    cross_add("cross1", 0)
                    layer_norm("ffn", 0)
                if quad == 29:
                    normalise("ffn", 0)
            gating(0)
            norms(1)
            self_add(1)
            layer_norm("cross1", 1)
            normalise("cross1", 1)
            softmax_in("cross1", 1)
            softmax_out("cross1", 1)
            cross_add("cross1", 1)
            layer_norm("ffn", 1)
            normalise("ffn", 1)
            gating(1)
            result(0)
            result(1)

        @block.tensor
        def _(pe):
            def transposes(kind, b):
                dst = bank[T_BANK[kind][b]]
                for t in range(T):
                    pe.wait_ge(xn_done[kind], T * b + t + 1)
                    last = pe.transpose(dst[:, P * t:P * t + P], xn[:, b, t], ident[:])
                last.then_inc(xT_mm[kind], 1)

            def cross_scores(kind, b):
                src, key = (xT, fold) if kind == "cross0" else (keyT, key2)
                if kind == "cross0":
                    pe.wait_ge(ld_xT[b], 16)
                    pe.wait_ge(fold_done, 1)
                else:
                    pe.wait_ge(key_done, b + 1)
                for t in range(T):
                    last = pe.matmul(bank[S_BANK[kind][b]][:, KV * t:KV * t + KV], src[:, b, P * t:P * t + P],
                                     key[:, KV * b:KV * b + KV], start=True, stop=True)
                last.then_inc(sc_mm[kind], 1)

            def cross_prT(kind, b):
                pe.wait_ge(pr_done[kind], b + 1)
                pe.transpose(bank[S_BANK[kind][b]][:, P:2 * P], pr[:, b].rearrange("p t k -> p (t k)"),
                             ident[:]).then_inc(prT_mm[kind], 1)

            def cross_av(kind, b):
                pe.wait_ge(prT_done[kind], b + 1)
                pe.matmul(bank[O_BANK[kind][b]][:], prT[:, b], ctx_bd[:, b].rearrange("p t d -> p (t d)"),
                          start=True, stop=True).then_inc(av_mm[kind], 1)

            def warm(n):
                for _ in range(n):
                    pe.matmul(bank[WARM_BANK][:], warm_src[:, 0:P], warm_src[:], start=True, stop=True)

            pe.wait_ge(warm_zero, 1)
            warm(WARM[0])
            pe.wait_ge(ld_first, 16)
            pe.matmul(bank[0][:, 0:B * KV], fw("wkT"), fw("ctxT"), start=True, stop=True).then_inc(keys_mm, 1)
            warm(WARM[1])
            pe.wait_ge(key0_done, 1)
            pe.wait_ge(wq0c_done, 1)
            pe.matmul(bank[7][:, 0:B * KV], wq0c[:], key0[:], start=True, stop=True)
            pe.matmul(bank[7][:, B * KV:2 * B * KV], fw("bq").broadcast_to([P, P]), key0[:],
                      start=True, stop=True).then_inc(fold_mm, 1)
            warm(WARM[2])
            for b in range(B):
                cross_scores("cross0", b)
            warm(WARM[3])
            pe.wait_ge(ld_rest, 16)
            pe.matmul(bank[5][:, 0:B * KV], rw("wxT"), fw("ctxT"), start=True, stop=True).then_inc(key2_mm, 1)
            pe.matmul(bank[6][:, 0:D], rw("woT"), rw("wff"), start=True, stop=True).then_inc(wof_mm, 1)
            pe.wait_ge(const_done, 1)
            for b in range(B):
                cross_prT("cross0", b)
            warm(WARM[4])
            pe.wait_ge(ld_ctx, 16 * T)
            for b in range(B):
                if b:
                    pe.wait_ge(key2_done, 1)
                cross_av("cross0", b)
            warm(WARM[5])

            def project_qk(b):
                pe.wait_ge(xT_done["self"], b + 1)
                pe.matmul(bank[Q_BANK[b]][:], rw("wq"), xT[:, b], start=True, stop=True).then_inc(q_mm, 1)
                pe.matmul(bank[K_BANK[b]][:], rw("wk"), xT[:, b], start=True, stop=True).then_inc(k_mm, 1)

            transposes("self", 0)
            project_qk(0)
            transposes("self", 1)
            project_qk(1)
            pe.wait_ge(prep_done, 1)
            for b in range(B):
                for t in range(T):
                    last = pe.matmul(bank[V_BANK[b]][:, D * t:D * t + D], xT[:, b, P * t:P * t + P], rw("wv"),
                                     start=True, stop=True)
                last.then_inc(v_mm, 1)
            warm(WARM[6])

            def scores(quad):
                for i in range(J * quad, J * quad + J):
                    b, g, kt, j = tile_of(i)
                    h = J * j + g
                    if i % (G * T * J) == 0:
                        if b == 0:
                            pe.wait_ge(r1_done, 2 * B)
                        pe.wait_ge(stacked[b], 16 * SLOTS)
                    if i == NSC - 1:
                        pe.wait_ge(v_done, B)
                    if i >= NSC:
                        pe.wait_ge(exp_done, i - NSC + 1)
                    if j < WARM_TILES:
                        pe.matmul(bank[SCORE_BANK[i % NSC]][:], warm_src[:, 0:P], warm_src[:], start=True, stop=True)
                    pe.matmul(bank[SCORE_BANK[i % NSC]][:], qks[ROWS * b:ROWS * b + ROWS, h, 1, P * kt:P * kt + P],
                              qks[ROWS * b:ROWS * b + ROWS, h, 0],
                              start=True, stop=True).then_inc(score_mm, 1)

            def values(quad):
                b, g, kt, _ = tile_of(J * quad)
                pe.wait_ge(vn_done, quad + 1)
                for j in range(J):
                    i = J * quad + j
                    last = pe.matmul(bank[OT_BANK[b]][32 * j:32 * j + 32, :], vn[:, g, J * kt + j], ex[:, i % NE],
                                     start=(g == 0 and kt == 0), stop=(g == G - 1 and kt == T - 1),
                                     skip_group_check=True)
                last.then_inc(pv_done, 1)

            def combine(b):
                pe.wait_ge(oT_done, b + 1)
                if b:
                    pe.wait_ge(exp_done, QUADS * J)
                for t in range(T):
                    at = (t % 2) * 2 * D
                    last = pe.matmul(bank[Z_BANK[b][t // 2]][:, at:at + 2 * D], oT[:, b, P * t:P * t + P], wof[:],
                                     start=True, stop=True)
                last.then_inc(z_mm, 1)

            def keys(b):
                pe.wait_ge(xT_done["cross1"], b + 1)
                pe.matmul(bank[KEY_BANK[b]][:], rw("wxT"), xT[:, b], start=True, stop=True).then_inc(key_mm, 1)

            def gate_logits(b):
                pe.wait_ge(xT_done["ffn"], b + 1)
                pe.matmul(bank[GATE_BANK[b]][:, 0:E], xsum[:, b:b + 1].broadcast_to([P, P]), rw("wg"),
                          start=True, stop=True).then_inc(logit_mm, 1)

            def turn_coef(b):
                pe.wait_ge(coef_done, b + 1)
                pe.matmul(bank[GATE_BANK[b]][0:E + 1, P:2 * P], coef[:, b], ident[:, 0:1].broadcast_to([P, P]),
                          start=True, stop=True).then_inc(coefT_mm, 1)

            UN = B * NETS * C

            def hidden(u):
                b, net, c = u // (NETS * C), u // C % NETS, u % C
                if c == 0 and net == 1:
                    pe.wait_ge(chosen, b + 1)
                if c == 0 and net == 0:
                    pe.wait_ge(xT_done["ffn"], b + 1)
                if u == 0:
                    pe.wait_ge(ld_w1, 32)
                    pe.wait_ge(exp_done, QUADS * J)
                if u >= 3:
                    pe.wait_ge(hid_done, u - 2)
                w = w1[:, P * c:P * c + P] if net == 0 else w1s[:, b, net - 1, P * c:P * c + P]
                pe.matmul(bank[H_BANK[u % 3]][:], w, x3T[:, b], start=True, stop=True).then_inc(hid_mm, 1)

            def project(u):
                b, net, c = u // (NETS * C), u // C % NETS, u % C
                acc = bank[ACC_BANK[b]]
                pe.wait_ge(hid_done, u + 1)
                if u == 0:
                    pe.wait_ge(main_scaled, 1)
                w = w2_main if net == 0 else w2s[:, b, net - 1]
                if net == NETS - 1 and c == 0:
                    if b == 0:
                        pe.wait_ge(ld_b2, 16)
                    pe.wait_ge(coefT_done, b + 1)
                    for t in range(T):
                        pe.matmul(acc[:, D * t:D * t + D], coefT[:, b], b2_sb[:], start=False, stop=False,
                                  skip_group_check=True)
                for t in range(T):
                    last = pe.matmul(acc[:, D * t:D * t + D], hid[:, u % 4, P * t:P * t + P],
                                     w[:, D * c:D * c + D], start=(net == 0 and c == 0 and t == 0),
                                     stop=(net == NETS - 1 and c == C - 1 and t == T - 1), skip_group_check=True)
                last.then_inc(hid_used, 1)

            def feed(u):
                if u < UN:
                    hidden(u)
                if u:
                    project(u - 1)

            for quad in range(QUADS):
                scores(quad)
                if quad >= PV_LAG:
                    values(quad - PV_LAG)
                if quad == 18:
                    combine(0)
                if quad == 23:
                    transposes("cross1", 0)
                if quad == 24:
                    keys(0)
                if quad == 25:
                    cross_scores("cross1", 0)
                if quad == 27:
                    cross_prT("cross1", 0)
                if quad == 28:
                    cross_av("cross1", 0)
                if quad == 30:
                    transposes("ffn", 0)
            values(QUADS - 2)
            gate_logits(0)
            feed(0)
            values(QUADS - 1)
            combine(1)
            feed(1)
            turn_coef(0)
            for u in range(2, UN + 1):
                feed(u)
                if u == 4:
                    transposes("cross1", 1)
                if u == 5:
                    keys(1)
                if u == 6:
                    cross_scores("cross1", 1)
                if u == 7:
                    cross_prT("cross1", 1)
                    cross_av("cross1", 1)
                if u == 10:
                    transposes("ffn", 1)
                    gate_logits(1)
                if u == 14:
                    turn_coef(1)


def kernel(**inputs):
    import numpy as np
    import concourse.bacc as bacc
    from concourse.bass_utils import run_bass_kernel_spmd

    a = {k: np.asarray(val) for k, val in inputs.items()}
    col = lambda n: a[n].reshape(-1, 1)
    by_row = lambda w: w.reshape(D, HEADS, DH).transpose(0, 2, 1).reshape(D, D)
    b1 = np.concatenate([a["L1_ffn_b1m"].reshape(1, H), a["L1_ffn_b1e"]]).reshape(E + 1, C, P)
    mask = np.zeros((B * KV, 4), np.uint8)
    mask[:, 0] = a["mask_BxS2_bf0"].reshape(B * KV).view(np.uint8)
    host = dict(
        x=a["x"],
        xt=a["x"].transpose(2, 0, 1),
        ctx=a["ctx_1024"],
        first=np.concatenate([a["L0_xattn_Wk"].T, a["L0_xattn_Wq"], a["ctx_1024"].reshape(B * KV, D).T,
                              col("L0_xattn_bk"), col("L0_xattn_bq")], axis=1),
        rest=np.concatenate([by_row(a["L0_ffn_Wq"]), by_row(a["L0_ffn_Wk"]), a["L0_ffn_Wv"], a["L0_ffn_Wo"], a["L0_ffn_Wo"].T,
                             a["L0_ffn_Wff"], a["L1_xattn_W"].T, a["L1_ffn_w_gate"], col("L1_xattn_b"),
                             col("L1_xattn_D"), b1.transpose(2, 0, 1).reshape(P, (E + 1) * C)], axis=1),
        w1m=a["L1_ffn_W1m"],
        w1e=a["L1_ffn_W1e"],
        w2m=a["L1_ffn_W2m"],
        w2e=a["L1_ffn_W2e"],
        b2=np.concatenate([a["L1_ffn_b2m"].reshape(1, D), a["L1_ffn_b2e"]]),
        row=np.concatenate([a["L1_ffn_b_gate"].reshape(1, E), a["L1_ffn_alpha"].reshape(1, 1)], axis=1),
        mask=mask.reshape(1, 4 * B * KV).view(np.int32),
    )
    nc = bacc.Bacc("TRN2", target_bir_lowering=False, num_devices=1)
    arrays, args = {}, []
    for name, arr in host.items():
        arr = np.ascontiguousarray(arr)
        arrays[f"in_{name}"] = arr
        args.append(nc.dram_tensor(f"in_{name}", arr.shape, mybir.dt.from_np(arr.dtype), kind="ExternalInput").ap())
    args.append(nc.dram_tensor("out_0", (B, S, D), F32, kind="ExternalOutput").ap())
    block_kernel(nc, *args)
    r = run_bass_kernel_spmd(nc, [arrays], core_ids=[0])
    return r.results[0]["out_0"]
```

```python
from contextlib import ExitStack

import concourse.bass as bass
from concourse import mybir

ALU = mybir.AluOpType
ACT = mybir.ActivationFunctionType
F32 = mybir.dt.float32
BF16 = mybir.dt.bfloat16
F32R = mybir.dt.float32r
I32 = mybir.dt.int32
HIGH_BITS = -(1 << 12)
U32 = mybir.dt.uint32
AX = mybir.AxisListType

P = 128
B, S, D = 2, 512, 128
T = S // P
KV = 32
HEADS, DH = 16, 8
G, J = 4, 4
E, H, C = 8, 512, 4
NETS = 3
LN_EPS = 1e-5
PARTS = 3
SLOTS = PARTS * PARTS - 1
ROWS = SLOTS * DH
PAIRS = [(0, 0), (0, 1), (1, 0), (1, 1), (0, 2), (1, 2), (2, 0), (2, 1)]
QK_SCALE = (-float(D) ** -0.5, 1.0)
SCORE_BANK = (0, 1, 2, 3, 7)
NSC = len(SCORE_BANK)
NE = 16
QUADS = B * G * T
PV_LAG = 2

WARM = (2, 5, 0, 5, 0, 17, 19)

WARM_TILES = 2

VALUES_AT = 3
ACT_AT = dict(squares=76, gelu_z=82, copy_xT1=94, relu_key=100, cross_exp=108, cross_prT=110, copy_xT2=120)
DVE_AT = dict(scale_w2=49, halve_w1=58, copy_oT=72, norms=82, self_add=86, normalise1=94, softmax_in=105, softmax_out=111, cross_add=117, normalise2=120)
PE_AT = dict(combine=76, transposes1=97, keys=100, cross_scores=105, cross_prT=114, cross_av=117, transposes2=122)
POOL_AT = dict(norm_z=18, rstd1=20, rstd2=27)
ACT_UNIT = dict(copy_oT=0, squares=0, gelu_z=2, copy_coefT0=2, copy_xT1=5, relu_key=5, cross_exp=6, cross_prT=6, copy_xT2=9, gate_exp=10, copy_coefT=14)
PE_STEP = dict(values_b=0, combine=0, turn_coef0=4, transposes1=10, keys=11, cross_scores=12, cross_prT=15, cross_av=15, transposes2=19, gate_logits=20, turn_coef=27)

FIRST = dict(wkT=(0, 128), wq0=(128, 128), ctxT=(256, 64), bk=(320, 1), bq=(321, 1))
FIRST_N = 322
REST = dict(wq=(0, 128), wk=(128, 128), wv=(256, 128), wo=(384, 128), woT=(512, 128), wff=(640, 128),
            wxT=(768, 128), wg=(896, E), bx=(904, 1), dx=(905, 1), b1=(906, (E + 1) * C))
REST_N = 906 + (E + 1) * C


def block_kernel(nc, x, xt, ctx, first, rest, w1m, w1e, w2m, w2e, b2, row, mask, out):
    with ExitStack() as stack:
        def sb(name, shape, dt=F32):
            return stack.enter_context(nc.sbuf_tensor(name, shape, dt))

        def sem(name):
            return stack.enter_context(nc.semaphore(name))

        bank = [stack.enter_context(nc.psum_tensor(f"bank{i}", [P, 512], F32)) for i in range(8)]

        ident = sb("ident", [P, P])
        minus_half = sb("minus_half", [P, T])
        minus_one = sb("minus_one", [P, J])
        iota_u = sb("iota_u", [P, E], mybir.dt.int32)
        iota_f = sb("iota_f", [P, E])
        first_sb = sb("first_sb", [P, FIRST_N])
        rest_sb = sb("rest_sb", [P, REST_N])
        ctx_bd = sb("ctx_bd", [P, B, T, D])
        w1 = sb("w1", [P, (E + 1) * H])
        w2 = sb("w2", [P, (E + 1) * H])
        b2_sb = sb("b2_sb", [E + 1, D])
        row_sb = sb("row_sb", [P, E + 1])
        mask_sb = sb("mask_sb", [P, B * KV], mybir.dt.int32)
        mask_bias = sb("mask_bias", [P, B * KV])
        a_sb = sb("a_sb", [P, 2])
        bk_scaled = sb("bk_scaled", [P, 1])
        wq0m = sb("wq0m", [P, 1])
        wq0c = sb("wq0c", [P, D])
        warm_src = sb("warm_src", [P, S], BF16)
        w2_main = sb("w2_main", [P, H])
        wof = sb("wof", [P, 2 * D])
        key0 = sb("key0", [P, B * KV])
        fold = sb("fold", [P, 2 * B * KV])
        key2 = sb("key2", [P, B * KV])

        def fw(name):
            at, n = FIRST[name]
            return first_sb[:, at:at + n]

        def rw(name):
            at, n = REST[name]
            return rest_sb[:, at:at + n]

        xr = sb("xr", [P, B, T, D])
        xn = sb("xn", [P, B, T, D])
        xT = sb("xT", [P, B, S])
        x3T = xn[:].rearrange("p b t d -> p b (t d)")
        stats = sb("stats", [P, B, T, 6])
        mv = sb("mv", [P, B, T, 2])
        veps = sb("veps", [P, B, T])
        rstd = sb("rstd", [P, B, T])
        sm = sb("sm", [P, B, T, KV])
        smx = sb("smx", [P, B, T])
        pr = sb("pr", [P, B, T, KV])
        prT = sb("prT", [P, B, P])
        keyT = sb("keyT", [P, B, S])
        early = sb("early", [P, 2, B, 2, S])
        left = early[:, 0]
        w2s = early[:, 1]
        x3h, x3l = sb("x3h", [P, B, S], F32R), sb("x3l", [P, B, S], F32R)
        w1mh, w1ml = sb("w1mh", [P, H], F32R), sb("w1ml", [P, H], F32R)
        w1sh, w1sl = sb("w1sh", [P, B, 2, H], F32R), sb("w1sl", [P, B, 2, H], F32R)
        parts = sb("parts", [P, B * 2 * PARTS * S], BF16)
        qkp = parts[:].rearrange("p (b c s) -> p b c s", b=B, c=2 * PARTS)
        hid = parts[:, 0:4 * 2 * S].bitcast(F32).rearrange("p (u s) -> p u s", u=4)
        qks = sb("qks", [B * ROWS, HEADS, 2, S], BF16)
        v = sb("v", [P, B, T, J, KV])
        vn = sb("vn", [P, G, T * J, KV])
        ex = sb("ex", [P, NE, S])
        neg_max = sb("neg_max", [P, QUADS * J])
        sums = sb("sums", [P, QUADS * J])
        rsum = sb("rsum", [P, QUADS * J])
        oT = parts[:, 4 * 2 * S:].bitcast(F32).rearrange("p (b s) -> p b s", b=B)
        sq = early[:, 1].rearrange("p b w (a d) -> p b (w a) d", d=D)
        ss = sb("ss", [P, B, T, 2])
        farg = sb("farg", [P, B, 2, T])
        fz = sb("fz", [P, B, T])
        gz = early[:, 0].rearrange("p b w (a d) -> p b (w a) d", d=D)[:, :, 0:T]
        xsum = sb("xsum", [P, B])
        logit = sb("logit", [P, B, E])
        lmax = sb("lmax", [P, B, 2])
        prob = sb("prob", [P, B, E])
        top = sb("top", [P, B, 8])
        top_i = sb("top_i", [P, B, 8], U32)
        top_f = sb("top_f", [P, B, 2])
        gate = sb("gate", [P, B, 4])
        coef = sb("coef", [P, B, E + 1])
        coef2 = sb("coef2", [P, B, E])
        coefT = sb("coefT", [E + 1, B, P])
        b1s = sb("b1s", [P, B, 2, C])
        res = xT[:].rearrange("p b (t d) -> p b t d", t=T)

        ld_first, ld_rest, ld_small = sem("ld_first"), sem("ld_rest"), sem("ld_small")
        ld_ctx, ld_w1, ld_w2, ld_b2 = sem("ld_ctx"), sem("ld_w1"), sem("ld_w2"), sem("ld_b2")
        ld_x = [sem(f"ld_x{b}") for b in range(B)]
        ld_xT = [sem(f"ld_xT{b}") for b in range(B)]
        rsum_done, vn_last_done = sem("rsum_done"), sem("vn_last_done")
        warm_zero, wq0c_done, main_scaled = sem("warm_zero"), sem("wq0c_done"), sem("main_scaled")
        w1_halved, x3_halved = sem("w1_halved"), sem("x3_halved")
        st_out = sem("st_out")
        const_done = sem("const_done")
        bd_zero = sem("bd_zero")
        pool_step = sem("pool_step")
        v_step = sem("v_step")
        a_step = sem("a_step")
        keys_mm, key0_done, fold_mm, fold_done, key2_mm, key2_done, wof_mm, prep_done = (
            sem(n) for n in ("keys_mm", "key0_done", "fold_mm", "fold_done", "key2_mm", "key2_done",
                             "wof_mm", "prep_done"))
        KINDS = ("cross0", "self", "cross1", "ffn")
        var_done = {k: sem(f"var_{k}") for k in KINDS}
        rstd_done = {k: sem(f"rstd_{k}") for k in KINDS}
        xn_done = {k: sem(f"xn_{k}") for k in KINDS}
        xT_mm = {k: sem(f"xT_mm_{k}") for k in KINDS}
        xT_done = {k: sem(f"xT_{k}") for k in KINDS}
        CROSS = ("cross0", "cross1")
        sc_mm = {k: sem(f"sc_mm_{k}") for k in CROSS}
        shifted = {k: sem(f"shifted_{k}") for k in CROSS}
        expd = {k: sem(f"expd_{k}") for k in CROSS}
        pr_done = {k: sem(f"pr_{k}") for k in CROSS}
        prT_mm = {k: sem(f"prT_mm_{k}") for k in CROSS}
        prT_done = {k: sem(f"prT_{k}") for k in CROSS}
        av_mm = {k: sem(f"av_mm_{k}") for k in CROSS}
        x_done = {k: sem(f"x_{k}") for k in CROSS}
        key_mm, key_done = sem("key_mm"), sem("key_done")
        q_mm, k_mm, v_mm = sem("q_mm"), sem("k_mm"), sem("v_mm")
        p1_done, r1_done, p2_done, p3_done = (sem(n) for n in ("p1_done", "r1_done", "p2_done", "p3_done"))
        v_done = sem("v_done")
        stacked = [sem(f"stacked{b}") for b in range(B)]
        score_mm, max_done, exp_done, vn_done, pv_done = (
            sem(n) for n in ("score_mm", "max_done", "exp_done", "vn_done", "pv_done"))
        oT_done, z_mm, sq_done, farg_done, fz_done, gelu_done = (
            sem(n) for n in ("oT_done", "z_mm", "sq_done", "farg_done", "fz_done", "gelu_done"))
        logit_mm, logit_done, pexp_done, coef_done, coefT_mm, coefT_done, chosen = (
            sem(n) for n in ("logit_mm", "logit_done", "pexp_done", "coef_done", "coefT_mm",
                             "coefT_done", "chosen"))
        hid_mm, hid_done, hid_used, res_done = (sem(n) for n in ("hid_mm", "hid_done", "hid_used", "res_done"))

        T_BANK = {"self": (0, 3), "cross1": (4, 5), "ffn": (4, 5)}
        S_BANK = {"cross0": (1, 4), "cross1": (4, 1)}
        O_BANK = {"cross0": (2, 5), "cross1": (6, 0)}
        Q_BANK, K_BANK, V_BANK = (1, 4), (2, 5), (6, 7)
        OT_BANK = (4, 5)
        Z_BANK = ((4, 6), (0, 1))
        KEY_BANK = (6, 0)
        GATE_BANK = (6, 1)
        H_BANK = (2, 3, 7)
        ACC_BANK = (4, 5)
        WARM_BANK = 3

        def tile_of(i):
            return i // (G * T * J), i // (T * J) % G, i // J % T, i % J

        block = stack.enter_context(nc.Block())

        @block.sync
        def _(sp):
            sp.dma_start(first_sb[:], first).then_inc(ld_first, 16)
            for b in range(B):
                sp.dma_start(xr[:, b], x[b].rearrange("(t p) d -> p t d", p=P)).then_inc(ld_x[b], 16)
                sp.dma_start(xT[:, b], xt[:, b]).then_inc(ld_xT[b], 16)
            sp.wait_ge(bd_zero, 1)
            for t in range(T):
                sp.dma_start(ctx_bd[KV * t:KV * t + KV, :, t, :],
                             ctx.rearrange("b k d -> k b d")).then_inc(ld_ctx, 16)
            sp.dma_start(rest_sb[:], rest).then_inc(ld_rest, 16)
            sp.dma_start(row_sb[:], row.broadcast_to([P, E + 1])).then_inc(ld_small, 16)
            sp.dma_start(mask_sb[:], mask.broadcast_to([P, B * KV])).then_inc(ld_small, 16)
            sp.dma_start(b2_sb[:], b2).then_inc(ld_b2, 16)
            part_done = (p1_done, p2_done, p3_done)
            for b in range(B):
                for n, (cq, ck) in enumerate(PAIRS):
                    sp.wait_ge(part_done[max(cq, ck)], 2 * b + 2)
                    step = PARTS + ck - cq
                    r = ROWS * b + DH * n
                    sp.dma_start(qks[r:r + DH], qkp[:, b, cq:PARTS + ck + 1:step]).then_inc(stacked[b], 16)
            sp.dma_start(w1[:, 0:H], w1m).then_inc(ld_w1, 16)
            sp.dma_start(w1[:, H:].rearrange("d (e h) -> d e h", e=E),
                         w1e.rearrange("e d h -> d e h")).then_inc(ld_w1, 16)
            sp.dma_start(w2[:, 0:H].rearrange("p (c d) -> p c d", c=C),
                         w2m.rearrange("(c p) d -> p c d", p=P)).then_inc(ld_w2, 16)
            sp.dma_start(w2[:, H:].rearrange("p (e d) -> p e d", e=E * C),
                         w2e.rearrange("e (c p) d -> p (e c) d", p=P)).then_inc(ld_w2, 16)
            for b in range(B):
                sp.wait_ge(res_done, b + 1)
                sp.dma_start(out[b].rearrange("(t p) d -> p t d", p=P), res[:, b]).then_inc(st_out, 16)
            sp.wait_ge(st_out, 16 * B)

        @block.gpsimd
        def _(pool):
            nc.gpsimd.memset(warm_src[:], 0.0).then_inc(warm_zero, 1)
            nc.gpsimd.memset(minus_half[:], -0.5)
            nc.gpsimd.memset(minus_one[:], -1.0)
            nc.gpsimd.memset(ident[:], 0.0).then_inc(pool_step, 1)
            nc.gpsimd.memset(ctx_bd[:], 0.0).then_inc(bd_zero, 1)
            pool.wait_ge(pool_step, 1)
            nc.gpsimd.affine_select(out=ident[:], in_=ident[:], compare_op=ALU.not_equal, fill=1.0, base=0,
                                    pattern=[[-1, P]], channel_multiplier=1).then_inc(const_done, 1)
            nc.gpsimd.iota(iota_u[:], pattern=[[1, E]], base=0, channel_multiplier=0).then_inc(const_done, 1)

            def rstd_of(kind, b):
                pool.wait_ge(var_done[kind], b + 1)
                nc.gpsimd.tensor_tensor(rstd[:, b], veps[:, b], minus_half[:], ALU.pow).then_inc(rstd_done[kind], 1)

            rstd_of("cross0", 0)
            rstd_of("cross0", 1)
            nc.gpsimd.memset(vn[:], 0.0).then_inc(const_done, 1)
            rstd_of("self", 0)
            rstd_of("self", 1)

            def norm_values(quad):
                b, g, kt, _ = tile_of(J * quad)
                if quad == 0:
                    pool.wait_ge(v_done, B)
                    pool.wait_ge(const_done, 3)
                if b:
                    pool.wait_ge(pv_done, quad - G * T + 1)
                a, z = J * quad, J * quad + J
                pool.wait_ge(exp_done, z)
                nc.gpsimd.tensor_tensor(rsum[:, a:z], sums[:, a:z], minus_one[:], ALU.pow).then_inc(rsum_done, 1)
                pool.wait_ge(rsum_done, quad + 1)
                nc.gpsimd.tensor_tensor(vn[:, g, J * kt:J * kt + J, DH * g:DH * g + DH],
                                        v[:, b, kt, :, DH * g:DH * g + DH],
                                        rsum[:, a:z].unsqueeze(2).broadcast_to([P, J, DH]),
                                        ALU.mult).then_inc(vn_done, 1)

            def norm_z(b):
                pool.wait_ge(farg_done, b + 1)
                nc.gpsimd.tensor_tensor(fz[:, b], farg[:, b, 1], minus_half[:], ALU.pow).then_inc(fz_done, 1)

            for quad in range(QUADS - 1):
                norm_values(quad)
                if quad == POOL_AT["norm_z"]:
                    norm_z(0)
                if quad == POOL_AT["rstd1"]:
                    rstd_of("cross1", 0)
                if quad == POOL_AT["rstd2"]:
                    rstd_of("ffn", 0)
            norm_z(1)
            rstd_of("cross1", 1)
            rstd_of("ffn", 1)

        @block.scalar
        def _(act):
            def copy_xT(kind, b):
                act.wait_ge(xT_mm[kind], b + 1)
                src = bank[T_BANK[kind][b]][:]
                if kind == "ffn":
                    nc.scalar.activation(x3T[:, b], src, ACT.Copy,
                                         accum_out=xsum[:, b:b + 1]).then_inc(xT_done[kind], 1)
                else:
                    nc.scalar.activation(xT[:, b], src, ACT.Copy).then_inc(xT_done[kind], 1)

            def cross_exp(kind, b):
                act.wait_ge(shifted[kind], b + 1)
                nc.scalar.activation(pr[:, b], sm[:, b], ACT.Exp).then_inc(expd[kind], 1)

            def cross_prT(kind, b):
                act.wait_ge(prT_mm[kind], b + 1)
                nc.scalar.activation(prT[:, b], bank[S_BANK[kind][b]][:, P:2 * P], ACT.Copy).then_inc(prT_done[kind], 1)

            def split(b):
                for which, ready, src in ((0, q_mm, Q_BANK), (1, k_mm, K_BANK)):
                    act.wait_ge(ready, b + 1)
                    nc.scalar.activation(qkp[:, b, PARTS * which], bank[src[b]][:], ACT.Copy,
                                         scale=QK_SCALE[which]).then_inc(p1_done, 1)

            def split_rest(b):
                for which in range(2):
                    act.wait_ge(r1_done, 2 * b + which + 1)
                    nc.scalar.activation(qkp[:, b, PARTS * which + 1], left[:, b, which], ACT.Copy).then_inc(p2_done, 1)

            def tile_exp(i):
                act.wait_ge(max_done, i + 1)
                if i >= NE:
                    act.wait_ge(pv_done, (i - NE) // J + 1)
                nc.scalar.activation(ex[:, i % NE], bank[SCORE_BANK[i % NSC]][:], ACT.Exp, bias=neg_max[:, i:i + 1],
                                     scale=-1.0, accum_out=sums[:, i:i + 1]).then_inc(exp_done, 1)

            def squares(b):
                act.wait_ge(z_mm, b + 1)
                for half in range(2):
                    nc.scalar.activation(sq[:, b, 4 * half:4 * half + 4].rearrange("p a d -> p (a d)"),
                                         bank[Z_BANK[b][half]][:], ACT.Square).then_inc(sq_done, 1)

            def gelu_z(b):
                act.wait_ge(fz_done, b + 1)
                for t in range(T):
                    at = (t % 2) * 2 * D + D
                    nc.scalar.activation(gz[:, b, t], bank[Z_BANK[b][t // 2]][:, at:at + D], ACT.Gelu,
                                         scale=fz[:, b, t:t + 1]).then_inc(gelu_done, 1)

            def relu_key(b):
                act.wait_ge(key_mm, b + 1)
                nc.scalar.activation(keyT[:, b], bank[KEY_BANK[b]][:], ACT.Relu, bias=rw("bx")).then_inc(key_done, 1)

            def gate_exp(b):
                act.wait_ge(logit_done, b + 1)
                nc.scalar.activation(prob[:, b], logit[:, b], ACT.Exp, bias=lmax[:, b, 0:1],
                                     accum_out=lmax[:, b, 1:2]).then_inc(pexp_done, 1)

            def copy_coefT(b):
                act.wait_ge(coefT_mm, b + 1)
                nc.scalar.activation(coefT[:, b], bank[GATE_BANK[b]][0:E + 1, P:2 * P], ACT.Copy).then_inc(coefT_done, 1)

            def hidden_gelu(u):
                b, net, c = u // (NETS * C), u // C % NETS, u % C
                act.wait_ge(hid_mm, u + 1)
                if u >= 4:
                    act.wait_ge(hid_used, u - 3)
                if net == 0:
                    bias = rw("b1")[:, c:c + 1]
                else:
                    act.wait_ge(chosen, b + 1)
                    bias = b1s[:, b, net - 1, c:c + 1]
                nc.scalar.activation(hid[:, u % 4], bank[H_BANK[u % 3]][:], ACT.Gelu_apprx_tanh,
                                     bias=bias).then_inc(hid_done, 1)

            act.wait_ge(ld_first, 16)
            nc.scalar.activation(bk_scaled[:], fw("bk"), ACT.Copy, scale=1.0 / 32.0).then_inc(a_step, 1)
            act.wait_ge(a_step, 1)
            act.wait_ge(keys_mm, 1)
            nc.scalar.activation(key0[:], bank[0][:, 0:B * KV], ACT.Identity, bias=bk_scaled[:, 0:1],
                                 scale=1.0 / 32.0).then_inc(key0_done, 1)
            act.wait_ge(fold_mm, 1)
            nc.scalar.activation(fold[:], bank[7][:, 0:2 * B * KV], ACT.Copy).then_inc(fold_done, 1)
            for b in range(B):
                cross_exp("cross0", b)
            for b in range(B):
                cross_prT("cross0", b)
            copy_xT("self", 0)
            split(0)
            copy_xT("self", 1)
            split_rest(0)
            split(1)
            split_rest(1)
            for b in range(B):
                act.wait_ge(v_mm, b + 1)
                nc.scalar.activation(v[:, b].rearrange("p t j c -> p (t j c)"), bank[V_BANK[b]][:], ACT.Copy).then_inc(v_done, 1)

            for i in range(QUADS * J):
                tile_exp(i)
                if i == ACT_AT["squares"]:
                    squares(0)
                if i == ACT_AT["gelu_z"]:
                    gelu_z(0)
                if i == ACT_AT["copy_xT1"]:
                    copy_xT("cross1", 0)
                if i == ACT_AT["relu_key"]:
                    relu_key(0)
                if i == ACT_AT["cross_exp"]:
                    cross_exp("cross1", 0)
                if i == ACT_AT["cross_prT"]:
                    cross_prT("cross1", 0)
                if i == ACT_AT["copy_xT2"]:
                    copy_xT("ffn", 0)
            gate_exp(0)
            for u in range(B * NETS * C):
                hidden_gelu(u)
                if u == ACT_UNIT["copy_oT"]:
                    act.wait_ge(pv_done, B * G * T)
                    nc.scalar.activation(oT[:, 1], bank[OT_BANK[1]][:], ACT.Copy).then_inc(oT_done, 1)
                if u == ACT_UNIT["squares"]:
                    squares(1)
                if u == ACT_UNIT["gelu_z"]:
                    gelu_z(1)
                if u == ACT_UNIT["copy_coefT0"]:
                    copy_coefT(0)
                if u == ACT_UNIT["copy_xT1"]:
                    copy_xT("cross1", 1)
                if u == ACT_UNIT["relu_key"]:
                    relu_key(1)
                if u == ACT_UNIT["cross_exp"]:
                    cross_exp("cross1", 1)
                if u == ACT_UNIT["cross_prT"]:
                    cross_prT("cross1", 1)
                if u == ACT_UNIT["copy_xT2"]:
                    copy_xT("ffn", 1)
                if u == ACT_UNIT["gate_exp"]:
                    gate_exp(1)
                if u == ACT_UNIT["copy_coefT"]:
                    copy_coefT(1)

        @block.vector
        def _(dve):
            links = [0]

            def link(ins):
                links[0] += 1
                ins.then_inc(v_step, 1)
                dve.wait_ge(v_step, links[0])

            def layer_norm(kind, b):
                if kind == "cross0":
                    dve.wait_ge(ld_x[b], 16)
                for t in range(T):
                    last = nc.vector.bn_stats(stats[:, b, t], xr[:, b, t])
                link(last)
                for t in range(T):
                    last = nc.vector.bn_aggr(mv[:, b, t], stats[:, b, t])
                link(last)
                nc.vector.tensor_scalar(veps[:, b], mv[:, b, :, 1], LN_EPS, None, ALU.add).then_inc(var_done[kind], 1)

            def normalise(kind, b):
                dve.wait_ge(rstd_done[kind], b + 1)
                for t in range(T):
                    nc.vector.tensor_scalar(xn[:, b, t], xr[:, b, t], mv[:, b, t, 0:1], rstd[:, b, t:t + 1],
                                            ALU.subtract, ALU.mult).then_inc(xn_done[kind], 1)

            def softmax_in(kind, b):
                if kind == "cross0" and b == 0:
                    dve.wait_ge(fold_done, 1)
                bias = fold[:, B * KV + KV * b:B * KV + KV * b + KV] if kind == "cross0" else mask_bias[:, KV * b:KV * b + KV]
                dve.wait_ge(sc_mm[kind], b + 1)
                ps = bank[S_BANK[kind][b]][:, 0:T * KV].rearrange("p (t k) -> p t k", t=T)
                if kind == "cross0":
                    dve.wait_ge(rstd_done[kind], b + 1)
                    link(nc.vector.tensor_tensor(sm[:, b], ps, rstd[:, b].unsqueeze(2).broadcast_to([P, T, KV]), ALU.mult))
                    ps = sm[:, b]
                link(nc.vector.tensor_tensor(sm[:, b], ps, bias.unsqueeze(1).broadcast_to([P, T, KV]), ALU.add))
                link(nc.vector.tensor_reduce(smx[:, b], sm[:, b], AX.X, ALU.max))
                nc.vector.tensor_tensor(sm[:, b], sm[:, b], smx[:, b].unsqueeze(2).broadcast_to([P, T, KV]),
                                        ALU.subtract).then_inc(shifted[kind], 1)

            def softmax_out(kind, b):
                dve.wait_ge(expd[kind], b + 1)
                link(nc.vector.tensor_reduce(smx[:, b], pr[:, b], AX.X, ALU.add))
                link(nc.vector.reciprocal(smx[:, b], smx[:, b]))
                nc.vector.tensor_tensor(pr[:, b], pr[:, b], smx[:, b].unsqueeze(2).broadcast_to([P, T, KV]),
                                        ALU.mult).then_inc(pr_done[kind], 1)

            def cross_add(kind, b):
                dve.wait_ge(av_mm[kind], b + 1)
                xf = xr[:, b].rearrange("p t d -> p (t d)")
                nc.vector.tensor_tensor(xf, bank[O_BANK[kind][b]][:], xf, ALU.add).then_inc(x_done[kind], 1)
                dve.wait_ge(x_done[kind], b + 1)

            def centre_wq0():
                dve.wait_ge(ld_first, 16)
                link(nc.vector.tensor_reduce(wq0m[:], fw("wq0"), AX.X, ALU.add))
                link(nc.vector.tensor_scalar(wq0m[:], wq0m[:], 1.0 / D, None, ALU.mult))
                nc.vector.tensor_scalar(wq0c[:], fw("wq0"), wq0m[:, 0:1], None, ALU.subtract).then_inc(wq0c_done, 1)

            def prep_rest():
                dve.wait_ge(ld_rest, 16)
                dve.wait_ge(key2_mm, 1)
                link(nc.vector.tensor_scalar(key2[:], bank[5][:, 0:B * KV], rw("bx"), 0.0, ALU.add, ALU.max))
                nc.vector.tensor_scalar(key2[:], key2[:], rw("dx"), None, ALU.mult).then_inc(key2_done, 1)
                nc.vector.tensor_copy(wof[:, 0:D], rw("wo"))
                dve.wait_ge(wof_mm, 1)
                nc.vector.tensor_copy(wof[:, D:], bank[6][:, 0:D]).then_inc(prep_done, 1)
                dve.wait_ge(ld_small, 32)
                nc.vector.tensor_scalar(mask_bias[:], mask_sb[:], -1e30, None, ALU.mult)
                link(nc.vector.tensor_scalar(a_sb[:, 0:1], row_sb[:, E:E + 1], 0.1, 1.0, ALU.max, ALU.min))
                nc.vector.tensor_scalar(a_sb[:, 1:2], a_sb[:, 0:1], -1.0, 1.0, ALU.mult, ALU.add)
                dve.wait_ge(const_done, 3)
                link(nc.vector.tensor_copy(iota_f[:], iota_u[:]))

            def split(b):
                for which, src in ((0, Q_BANK), (1, K_BANK)):
                    dve.wait_ge(p1_done, 2 * b + which + 1)
                    nc.vector.scalar_tensor_tensor(left[:, b, which], bank[src[b]][:], QK_SCALE[which],
                                                   qkp[:, b, PARTS * which], ALU.mult, ALU.subtract).then_inc(r1_done, 1)
                for which in range(2):
                    dve.wait_ge(p2_done, 2 * b + which + 1)
                    nc.vector.tensor_tensor(qkp[:, b, PARTS * which + 2], left[:, b, which],
                                            qkp[:, b, PARTS * which + 1], ALU.subtract).then_inc(p3_done, 1)

            def halve(high, low, src, tmp):
                link(nc.vector.tensor_scalar(tmp.bitcast(I32), src.bitcast(I32), HIGH_BITS, None, ALU.bitwise_and))
                nc.vector.tensor_copy(high, tmp)
                return nc.vector.tensor_tensor(low, src, tmp, ALU.subtract)

            def tile_max(i):
                dve.wait_ge(score_mm, i + 1)
                nc.vector.tensor_reduce(neg_max[:, i:i + 1], bank[SCORE_BANK[i % NSC]][:], AX.X, ALU.min).then_inc(max_done, 1)

            def norm_last_values():
                quad = QUADS - 1
                b, g, kt, _ = tile_of(J * quad)
                dve.wait_ge(pv_done, quad - G * T + 1)
                a, z = J * quad, J * quad + J
                dve.wait_ge(exp_done, z)
                link(nc.vector.reciprocal(rsum[:, a:z], sums[:, a:z]))
                nc.vector.tensor_tensor(vn[:, g, J * kt:J * kt + J, DH * g:DH * g + DH],
                                        v[:, b, kt, :, DH * g:DH * g + DH],
                                        rsum[:, a:z].unsqueeze(2).broadcast_to([P, J, DH]),
                                        ALU.mult).then_inc(vn_last_done, 1)

            def norms(b):
                for half in range(2):
                    dve.wait_ge(sq_done, 2 * b + half + 1)
                    last = nc.vector.tensor_reduce(ss[:, b].rearrange("p t c -> p (t c)")[:, T * half:T * half + T],
                                                   sq[:, b, T * half:T * half + T], AX.X, ALU.add)
                link(last)
                link(nc.vector.tensor_scalar(farg[:, b, 0], ss[:, b, :, 0], 1e-24, 1e-24, ALU.max, ALU.mult))
                nc.vector.scalar_tensor_tensor(farg[:, b, 1], farg[:, b, 0], 1e-37, ss[:, b, :, 1],
                                               ALU.max, ALU.max).then_inc(farg_done, 1)

            def self_add(b):
                for t in range(T):
                    dve.wait_ge(gelu_done, T * b + t + 1)
                    last = nc.vector.tensor_tensor(xr[:, b, t], xr[:, b, t], gz[:, b, t], ALU.add)
                link(last)

            def halve_x3(b):
                dve.wait_ge(xT_done["ffn"], b + 1)
                halve(x3h[:, b], x3l[:, b], x3T[:, b], keyT[:, b]).then_inc(x3_halved, 1)

            def gating(b):
                dve.wait_ge(logit_mm, b + 1)
                link(nc.vector.scalar_tensor_tensor(logit[:, b], bank[GATE_BANK[b]][:, 0:E], 1.0 / S, row_sb[:, 0:E],
                                                    ALU.mult, ALU.add))
                nc.vector.tensor_reduce(lmax[:, b, 0:1], logit[:, b], AX.X, ALU.max, negate=True).then_inc(logit_done, 1)
                dve.wait_ge(pexp_done, b + 1)
                link(nc.vector.reciprocal(gate[:, b, 0:1], lmax[:, b, 1:2]))
                link(nc.vector.tensor_scalar(prob[:, b], prob[:, b], gate[:, b, 0:1], None, ALU.mult))
                link(nc.vector.max(top[:, b], prob[:, b]))
                link(nc.vector.max_index(top_i[:, b], top[:, b], prob[:, b]))
                nc.vector.tensor_copy(top_f[:, b], top_i[:, b, 0:2])
                link(nc.vector.tensor_tensor(gate[:, b, 1:2], top[:, b, 0:1], top[:, b, 1:2], ALU.add))
                link(nc.vector.reciprocal(gate[:, b, 1:2], gate[:, b, 1:2]))
                link(nc.vector.tensor_scalar(gate[:, b, 2:4], top[:, b, 0:2], gate[:, b, 1:2], a_sb[:, 1:2],
                                             ALU.mult, ALU.mult))
                nc.vector.tensor_copy(coef[:, b, 0:1], a_sb[:, 0:1])
                nc.vector.tensor_scalar(coef[:, b, 1:], iota_f[:], top_f[:, b, 0:1], gate[:, b, 2:3],
                                        ALU.is_equal, ALU.mult)
                link(nc.vector.tensor_scalar(coef2[:, b], iota_f[:], top_f[:, b, 1:2], gate[:, b, 3:4],
                                             ALU.is_equal, ALU.mult))
                nc.vector.tensor_tensor(coef[:, b, 1:], coef[:, b, 1:], coef2[:, b], ALU.add).then_inc(coef_done, 1)
                if b == 0:
                    dve.wait_ge(ld_w1, 32)
                    dve.wait_ge(ld_w2, 32)
                for k in range(2):
                    e = dve.value_load(top_i[0:1, b, k:k + 1], min_val=0, max_val=E - 1)
                    halve(w1sh[:, b, k], w1sl[:, b, k], w1[:, bass.ds(e * H + H, H)], (keyT, xT)[k][:, b])
                    nc.vector.tensor_scalar(w2s[:, b, k], w2[:, bass.ds(e * H + H, H)], gate[:, b, 2 + k:3 + k], None,
                                            ALU.mult)
                    last = nc.vector.tensor_copy(b1s[:, b, k], rest_sb[:, bass.ds(e * C + REST["b1"][0] + C, C)])
                last.then_inc(chosen, 1)

            def result(b):
                dve.wait_ge(hid_used, (b + 1) * NETS * C)
                nc.vector.tensor_tensor(res[:, b].rearrange("p t d -> p (t d)"), bank[ACC_BANK[b]][:],
                                        xr[:, b].rearrange("p t d -> p (t d)"), ALU.add).then_inc(res_done, 1)

            centre_wq0()
            for b in range(B):
                layer_norm("cross0", b)
            for b in range(B):
                softmax_in("cross0", b)
            for b in range(B):
                softmax_out("cross0", b)
            prep_rest()
            cross_add("cross0", 0)
            layer_norm("self", 0)
            cross_add("cross0", 1)
            normalise("self", 0)
            layer_norm("self", 1)
            normalise("self", 1)
            for b in range(B):
                split(b)

            for i in range(QUADS * J):
                tile_max(i)
                if i == DVE_AT["scale_w2"]:
                    dve.wait_ge(ld_w2, 32)
                    nc.vector.tensor_scalar(w2_main[:], w2[:, 0:H], a_sb[:, 0:1], None, ALU.mult).then_inc(main_scaled, 1)
                if i == DVE_AT["halve_w1"]:
                    dve.wait_ge(ld_w1, 32)
                    halve(w1mh[:], w1ml[:], w1[:, 0:H], keyT[:, 1]).then_inc(w1_halved, 1)
                if i == DVE_AT["copy_oT"]:
                    dve.wait_ge(pv_done, G * T)
                    nc.vector.tensor_copy(oT[:, 0], bank[OT_BANK[0]][:]).then_inc(oT_done, 1)
                if i == DVE_AT["norms"]:
                    norms(0)
                if i == DVE_AT["self_add"]:
                    self_add(0)
                    layer_norm("cross1", 0)
                if i == DVE_AT["normalise1"]:
                    normalise("cross1", 0)
                if i == DVE_AT["softmax_in"]:
                    softmax_in("cross1", 0)
                if i == DVE_AT["softmax_out"]:
                    softmax_out("cross1", 0)
                if i == DVE_AT["cross_add"]:
                    cross_add("cross1", 0)
                    layer_norm("ffn", 0)
                if i == DVE_AT["normalise2"]:
                    normalise("ffn", 0)
            halve_x3(0)
            norm_last_values()
            gating(0)
            norms(1)
            self_add(1)
            layer_norm("cross1", 1)
            normalise("cross1", 1)
            softmax_in("cross1", 1)
            softmax_out("cross1", 1)
            cross_add("cross1", 1)
            layer_norm("ffn", 1)
            normalise("ffn", 1)
            halve_x3(1)
            gating(1)
            result(0)
            result(1)

        @block.tensor
        def _(pe):
            def transposes(kind, b):
                dst = bank[T_BANK[kind][b]]
                for t in range(T):
                    pe.wait_ge(xn_done[kind], T * b + t + 1)
                    last = pe.transpose(dst[:, P * t:P * t + P], xn[:, b, t], ident[:])
                last.then_inc(xT_mm[kind], 1)

            def cross_scores(kind, b):
                src, key = (xT, fold) if kind == "cross0" else (keyT, key2)
                if kind == "cross0":
                    pe.wait_ge(ld_xT[b], 16)
                    pe.wait_ge(fold_done, 1)
                else:
                    pe.wait_ge(key_done, b + 1)
                for t in range(T):
                    last = pe.matmul(bank[S_BANK[kind][b]][:, KV * t:KV * t + KV], src[:, b, P * t:P * t + P],
                                     key[:, KV * b:KV * b + KV], start=True, stop=True)
                last.then_inc(sc_mm[kind], 1)

            def cross_prT(kind, b):
                pe.wait_ge(pr_done[kind], b + 1)
                pe.transpose(bank[S_BANK[kind][b]][:, P:2 * P], pr[:, b].rearrange("p t k -> p (t k)"),
                             ident[:]).then_inc(prT_mm[kind], 1)

            def cross_av(kind, b):
                pe.wait_ge(prT_done[kind], b + 1)
                pe.matmul(bank[O_BANK[kind][b]][:], prT[:, b], ctx_bd[:, b].rearrange("p t d -> p (t d)"),
                          start=True, stop=True).then_inc(av_mm[kind], 1)

            def warm(n):
                for _ in range(n):
                    pe.matmul(bank[WARM_BANK][:], warm_src[:, 0:P], warm_src[:], start=True, stop=True)

            pe.wait_ge(warm_zero, 1)
            warm(WARM[0])
            pe.wait_ge(ld_first, 16)
            pe.matmul(bank[0][:, 0:B * KV], fw("wkT"), fw("ctxT"), start=True, stop=True).then_inc(keys_mm, 1)
            warm(WARM[1])
            pe.wait_ge(key0_done, 1)
            pe.wait_ge(wq0c_done, 1)
            pe.matmul(bank[7][:, 0:B * KV], wq0c[:], key0[:], start=True, stop=True)
            pe.matmul(bank[7][:, B * KV:2 * B * KV], fw("bq").broadcast_to([P, P]), key0[:],
                      start=True, stop=True).then_inc(fold_mm, 1)
            warm(WARM[2])
            for b in range(B):
                cross_scores("cross0", b)
            warm(WARM[3])
            pe.wait_ge(ld_rest, 16)
            pe.matmul(bank[5][:, 0:B * KV], rw("wxT"), fw("ctxT"), start=True, stop=True).then_inc(key2_mm, 1)
            pe.matmul(bank[6][:, 0:D], rw("woT"), rw("wff"), start=True, stop=True).then_inc(wof_mm, 1)
            pe.wait_ge(const_done, 1)
            for b in range(B):
                cross_prT("cross0", b)
            warm(WARM[4])
            pe.wait_ge(ld_ctx, 16 * T)
            for b in range(B):
                if b:
                    pe.wait_ge(key2_done, 1)
                cross_av("cross0", b)
            warm(WARM[5])

            def project_qk(b):
                pe.wait_ge(xT_done["self"], b + 1)
                pe.matmul(bank[Q_BANK[b]][:], rw("wq"), xT[:, b], start=True, stop=True).then_inc(q_mm, 1)
                pe.matmul(bank[K_BANK[b]][:], rw("wk"), xT[:, b], start=True, stop=True).then_inc(k_mm, 1)

            transposes("self", 0)
            project_qk(0)
            transposes("self", 1)
            project_qk(1)
            pe.wait_ge(prep_done, 1)
            for b in range(B):
                for t in range(T):
                    last = pe.matmul(bank[V_BANK[b]][:, D * t:D * t + D], xT[:, b, P * t:P * t + P], rw("wv"),
                                     start=True, stop=True)
                last.then_inc(v_mm, 1)
            warm(WARM[6])

            def tile_scores(i):
                b, g, kt, j = tile_of(i)
                h = J * j + g
                if i % (G * T * J) == 0:
                    if b == 0:
                        pe.wait_ge(r1_done, 2 * B)
                    pe.wait_ge(stacked[b], 16 * SLOTS)
                if i == NSC - 1:
                    pe.wait_ge(v_done, B)
                if i >= NSC:
                    pe.wait_ge(exp_done, i - NSC + 1)
                if j < WARM_TILES:
                    pe.matmul(bank[SCORE_BANK[i % NSC]][:], warm_src[:, 0:P], warm_src[:], start=True, stop=True)
                pe.matmul(bank[SCORE_BANK[i % NSC]][:], qks[ROWS * b:ROWS * b + ROWS, h, 1, P * kt:P * kt + P],
                          qks[ROWS * b:ROWS * b + ROWS, h, 0],
                          start=True, stop=True).then_inc(score_mm, 1)

            def values(quad):
                b, g, kt, _ = tile_of(J * quad)
                if quad < QUADS - 1:
                    pe.wait_ge(vn_done, quad + 1)
                else:
                    pe.wait_ge(vn_last_done, 1)
                for j in range(J):
                    i = J * quad + j
                    last = pe.matmul(bank[OT_BANK[b]][32 * j:32 * j + 32, :], vn[:, g, J * kt + j], ex[:, i % NE],
                                     start=(g == 0 and kt == 0), stop=(g == G - 1 and kt == T - 1),
                                     skip_group_check=True)
                last.then_inc(pv_done, 1)

            def combine(b):
                pe.wait_ge(oT_done, b + 1)
                if b:
                    pe.wait_ge(exp_done, QUADS * J)
                for t in range(T):
                    at = (t % 2) * 2 * D
                    last = pe.matmul(bank[Z_BANK[b][t // 2]][:, at:at + 2 * D], oT[:, b, P * t:P * t + P], wof[:],
                                     start=True, stop=True)
                last.then_inc(z_mm, 1)

            def keys(b):
                pe.wait_ge(xT_done["cross1"], b + 1)
                pe.matmul(bank[KEY_BANK[b]][:], rw("wxT"), xT[:, b], start=True, stop=True).then_inc(key_mm, 1)

            def gate_logits(b):
                pe.wait_ge(xT_done["ffn"], b + 1)
                pe.matmul(bank[GATE_BANK[b]][:, 0:E], xsum[:, b:b + 1].broadcast_to([P, P]), rw("wg"),
                          start=True, stop=True).then_inc(logit_mm, 1)

            def turn_coef(b):
                pe.wait_ge(coef_done, b + 1)
                pe.matmul(bank[GATE_BANK[b]][0:E + 1, P:2 * P], coef[:, b], ident[:, 0:1].broadcast_to([P, P]),
                          start=True, stop=True).then_inc(coefT_mm, 1)

            UN = B * NETS * C

            def hidden(u):
                b, net, c = u // (NETS * C), u // C % NETS, u % C
                if c == 0 and net == 1:
                    pe.wait_ge(chosen, b + 1)
                if c == 0 and net == 0:
                    pe.wait_ge(x3_halved, b + 1)
                if u == 0:
                    pe.wait_ge(w1_halved, 1)
                    pe.wait_ge(exp_done, QUADS * J)
                if u >= 3:
                    pe.wait_ge(hid_done, u - 2)
                cols = slice(P * c, P * c + P)
                wh, wl = (w1mh[:, cols], w1ml[:, cols]) if net == 0 else (w1sh[:, b, net - 1, cols], w1sl[:, b, net - 1, cols])
                dst = bank[H_BANK[u % 3]][:]
                pe.matmul(dst, wl, x3h[:, b], start=True, stop=False)
                pe.matmul(dst, wh, x3l[:, b], start=False, stop=False)
                pe.matmul(dst, wh, x3h[:, b], start=False, stop=True).then_inc(hid_mm, 1)

            def project(u):
                b, net, c = u // (NETS * C), u // C % NETS, u % C
                acc = bank[ACC_BANK[b]]
                pe.wait_ge(hid_done, u + 1)
                if u == 0:
                    pe.wait_ge(main_scaled, 1)
                w = w2_main if net == 0 else w2s[:, b, net - 1]
                if net == NETS - 1 and c == 0:
                    if b == 0:
                        pe.wait_ge(ld_b2, 16)
                    pe.wait_ge(coefT_done, b + 1)
                    for t in range(T):
                        pe.matmul(acc[:, D * t:D * t + D], coefT[:, b], b2_sb[:], start=False, stop=False,
                                  skip_group_check=True)
                for t in range(T):
                    last = pe.matmul(acc[:, D * t:D * t + D], hid[:, u % 4, P * t:P * t + P],
                                     w[:, D * c:D * c + D], start=(net == 0 and c == 0 and t == 0),
                                     stop=(net == NETS - 1 and c == C - 1 and t == T - 1), skip_group_check=True)
                last.then_inc(hid_used, 1)

            def feed(step):
                u = step // 2
                if step % 2 == 0 and u < UN:
                    hidden(u)
                elif step % 2 and u:
                    project(u - 1)

            for i in range(QUADS * J):
                tile_scores(i)
                if i >= J * PV_LAG + VALUES_AT and (i - VALUES_AT) % J == 0:
                    values((i - VALUES_AT) // J - PV_LAG)
                if i == PE_AT["combine"]:
                    combine(0)
                if i == PE_AT["transposes1"]:
                    transposes("cross1", 0)
                if i == PE_AT["keys"]:
                    keys(0)
                if i == PE_AT["cross_scores"]:
                    cross_scores("cross1", 0)
                if i == PE_AT["cross_prT"]:
                    cross_prT("cross1", 0)
                if i == PE_AT["cross_av"]:
                    cross_av("cross1", 0)
                if i == PE_AT["transposes2"]:
                    transposes("ffn", 0)
            values(QUADS - 2)
            gate_logits(0)
            for step in range(2 * UN + 2):
                feed(step)
                if step == PE_STEP["values_b"]:
                    values(QUADS - 1)
                if step == PE_STEP["combine"]:
                    combine(1)
                if step == PE_STEP["turn_coef0"]:
                    turn_coef(0)
                if step == PE_STEP["transposes1"]:
                    transposes("cross1", 1)
                if step == PE_STEP["keys"]:
                    keys(1)
                if step == PE_STEP["cross_scores"]:
                    cross_scores("cross1", 1)
                if step == PE_STEP["cross_prT"]:
                    cross_prT("cross1", 1)
                if step == PE_STEP["cross_av"]:
                    cross_av("cross1", 1)
                if step == PE_STEP["transposes2"]:
                    transposes("ffn", 1)
                if step == PE_STEP["gate_logits"]:
                    gate_logits(1)
                if step == PE_STEP["turn_coef"]:
                    turn_coef(1)


def kernel(**inputs):
    import numpy as np
    import concourse.bacc as bacc
    from concourse.bass_utils import run_bass_kernel_spmd

    a = {k: np.asarray(val) for k, val in inputs.items()}
    col = lambda n: a[n].reshape(-1, 1)
    by_row = lambda w: w.reshape(D, HEADS, DH).transpose(0, 2, 1).reshape(D, D)
    b1 = np.concatenate([a["L1_ffn_b1m"].reshape(1, H), a["L1_ffn_b1e"]]).reshape(E + 1, C, P)
    mask = np.zeros((B * KV, 4), np.uint8)
    mask[:, 0] = a["mask_BxS2_bf0"].reshape(B * KV).view(np.uint8)
    host = dict(
        x=a["x"],
        xt=a["x"].transpose(2, 0, 1),
        ctx=a["ctx_1024"],
        first=np.concatenate([a["L0_xattn_Wk"].T, a["L0_xattn_Wq"], a["ctx_1024"].reshape(B * KV, D).T,
                              col("L0_xattn_bk"), col("L0_xattn_bq")], axis=1),
        rest=np.concatenate([by_row(a["L0_ffn_Wq"]), by_row(a["L0_ffn_Wk"]), a["L0_ffn_Wv"], a["L0_ffn_Wo"], a["L0_ffn_Wo"].T,
                             a["L0_ffn_Wff"], a["L1_xattn_W"].T, a["L1_ffn_w_gate"], col("L1_xattn_b"),
                             col("L1_xattn_D"), b1.transpose(2, 0, 1).reshape(P, (E + 1) * C)], axis=1),
        w1m=a["L1_ffn_W1m"],
        w1e=a["L1_ffn_W1e"],
        w2m=a["L1_ffn_W2m"],
        w2e=a["L1_ffn_W2e"],
        b2=np.concatenate([a["L1_ffn_b2m"].reshape(1, D), a["L1_ffn_b2e"]]),
        row=np.concatenate([a["L1_ffn_b_gate"].reshape(1, E), a["L1_ffn_alpha"].reshape(1, 1)], axis=1),
        mask=mask.reshape(1, 4 * B * KV).view(np.int32),
    )
    nc = bacc.Bacc("TRN2", target_bir_lowering=False, num_devices=1)
    arrays, args = {}, []
    for name, arr in host.items():
        arr = np.ascontiguousarray(arr)
        arrays[f"in_{name}"] = arr
        args.append(nc.dram_tensor(f"in_{name}", arr.shape, mybir.dt.from_np(arr.dtype), kind="ExternalInput").ap())
    args.append(nc.dram_tensor("out_0", (B, S, D), F32, kind="ExternalOutput").ap())
    block_kernel(nc, *args)
    r = run_bass_kernel_spmd(nc, [arrays], core_ids=[0])
    return r.results[0]["out_0"]
```
